# Optimizing a Trainium2 kernel written in Bass

```python
import numpy as np
import jax
import jax.numpy as jnp

def _softmax(x, axis=-1):
    return jax.nn.softmax(x, axis=axis)

def _gelu(x):
    return jax.nn.gelu(x, approximate=True)

def _silu(x):
    return jax.nn.silu(x)

def _sigmoid(x):
    return jax.nn.sigmoid(x)

def _layernorm(x, axis=-1, eps=1e-05):
    m = jnp.mean(x, axis=axis, keepdims=True)
    v = jnp.var(x, axis=axis, keepdims=True)
    return (x - m) / jnp.sqrt(v + eps)

def _scatter_add(tgt, idx, src, axis=0):
    return tgt.at[idx].add(src)

def _segment_sum(src, seg, n):
    return jax.ops.segment_sum(src, seg, n)
kernel_name = 'mk_vit_tower_d2_tok_img2048_r4_199e05'

def setup_inputs(seed: int=0):
    np.random.seed(seed)
    _w = jnp.asarray

    def _rec_inputs():
        import jax
        import jax.numpy as jnp
        _rk = jax.random.key(seed)
        x = -0.00340659 + 1.00146 * jax.random.normal(jax.random.fold_in(_rk, 1), (16, 256, 64, 2), jnp.float32)
        return x
    x = _rec_inputs()

    def _L0_tok_setup():
        import jax, jax.numpy as jnp
        import numpy as np
        CH, H, N, N_SSM, SEQ_L = (1, 256, 64, 256, 512)

        def _kernel(C_ri, log_dt, B_ri, inv_A_real, A_imag, L):
            C = C_ri[..., 0] + 1j * C_ri[..., 1]
            B = B_ri[..., 0] + 1j * B_ri[..., 1]
            A = -jnp.exp(inv_A_real) + 1j * A_imag
            rep = log_dt.shape[0] // inv_A_real.shape[0]
            B = jnp.tile(B, (rep, 1))
            A = jnp.tile(A, (rep, 1))
            dt = jnp.exp(log_dt)
            dtA = A * dt[:, None]
            Ct = B[None] * C / (1.0 - dtA / 2) * dt[:, None]
            dA = (1.0 + dtA / 2) / (1.0 - dtA / 2)
            dA_log = jnp.log(dA)
            l = jnp.arange(L, dtype=jnp.float32)
            V = jnp.exp(dA_log[:, :, None] * l)
            K = 2.0 * jnp.einsum('chn,hnl->chl', Ct, V).real
            return K
        key = jax.random.key(seed)
        ks = jax.random.split(key, 5)
        return {'C_ri': jax.random.normal(ks[0], (CH, H, N, 2), dtype=jnp.float32), 'log_dt': jax.random.normal(ks[1], (H,), dtype=jnp.float32), 'B_ri': jax.random.normal(ks[2], (N_SSM, N, 2), dtype=jnp.float32), 'inv_A_real': jax.random.normal(ks[3], (N_SSM, N), dtype=jnp.float32), 'A_imag': jax.random.normal(ks[4], (N_SSM, N), dtype=jnp.float32), 'L': SEQ_L}
    _L0_tok_all = _L0_tok_setup()
    _L0_tok_in = {k: v for k, v in _L0_tok_all.items() if k in ('log_dt', 'B_ri', 'inv_A_real', 'A_imag')}
    del _L0_tok_all

    def _L0_attn_setup():
        import jax, jax.numpy as jnp
        import numpy as np
        D_MODEL = 512
        NUM_HEADS = 16
        D_K = D_MODEL // NUM_HEADS

        def _heads(t, B, S):
            return t.reshape(B, S, NUM_HEADS, D_K).transpose(0, 2, 1, 3)
        key = jax.random.key(seed)
        ks = jax.random.split(key, 9)
        s = 1.0 / np.sqrt(D_MODEL)
        x = jax.random.normal(ks[0], (4, 1024, D_MODEL), dtype=jnp.float32)
        wq = jax.random.uniform(ks[1], (D_MODEL, D_MODEL), jnp.float32, -s, s)
        bq = jax.random.uniform(ks[2], (D_MODEL,), jnp.float32, -s, s)
        wk = jax.random.uniform(ks[3], (D_MODEL, D_MODEL), jnp.float32, -s, s)
        bk = jax.random.uniform(ks[4], (D_MODEL,), jnp.float32, -s, s)
        wv = jax.random.uniform(ks[5], (D_MODEL, D_MODEL), jnp.float32, -s, s)
        bv = jax.random.uniform(ks[6], (D_MODEL,), jnp.float32, -s, s)
        wo = jax.random.uniform(ks[7], (D_MODEL, D_MODEL), jnp.float32, -s, s)
        bo = jax.random.uniform(ks[8], (D_MODEL,), jnp.float32, -s, s)
        return {'x': x, 'wq': wq, 'bq': bq, 'wk': wk, 'bk': bk, 'wv': wv, 'bv': bv, 'wo': wo, 'bo': bo}
    _L0_attn_all = _L0_attn_setup()
    _L0_attn_in = {k: v for k, v in _L0_attn_all.items() if k in ('wq', 'bq', 'wk', 'bk', 'wv', 'bv', 'wo', 'bo')}
    del _L0_attn_all

    def _L0_ffn_setup():
        import jax, jax.numpy as jnp
        import numpy as np
        B, S, D = (4, 1024, 512)
        DFF = 4 * D
        SKIP = 0.125
        key = jax.random.key(seed)
        ks = jax.random.split(key, 4)
        s_in = 1.0 / np.sqrt(D).astype(np.float32)
        s_ff = 1.0 / np.sqrt(DFF).astype(np.float32)
        return {'x': jax.random.normal(ks[0], (B, S, D), jnp.float32), 'Wr': jax.random.normal(ks[1], (D, 1), jnp.float32) * s_in, 'br': jnp.zeros((1,), jnp.float32), 'W1': jax.random.normal(ks[2], (D, DFF), jnp.float32) * s_in, 'b1': jnp.zeros((DFF,), jnp.float32), 'W2': jax.random.normal(ks[3], (DFF, D), jnp.float32) * s_ff, 'b2': jnp.zeros((D,), jnp.float32)}
    _L0_ffn_all = _L0_ffn_setup()
    _L0_ffn_in = {k: v for k, v in _L0_ffn_all.items() if k in ('Wr', 'br', 'W1', 'b1', 'W2', 'b2')}
    del _L0_ffn_all

    def _L1_attn_setup():
        import jax, jax.numpy as jnp
        import numpy as np
        STATE_SIZE = 16
        HIDDEN = 512
        DT_RANK = 64
        BATCH = 2
        SEQ = 512
        key = jax.random.key(seed)
        ks = jax.random.split(key, 8)
        scale = lambda fan_in: 1.0 / np.sqrt(fan_in)
        inp = {'input': jax.random.normal(ks[0], (BATCH, SEQ, HIDDEN), dtype=jnp.float32), 'W_dt_in': jax.random.uniform(ks[1], (DT_RANK, HIDDEN), jnp.float32, -scale(HIDDEN), scale(HIDDEN)), 'W_dt_out': jax.random.uniform(ks[2], (HIDDEN, DT_RANK), jnp.float32, -scale(DT_RANK), scale(DT_RANK)), 'b_dt_out': jax.random.uniform(ks[3], (HIDDEN,), jnp.float32, -scale(DT_RANK), scale(DT_RANK)), 'W_B': jax.random.uniform(ks[4], (STATE_SIZE, HIDDEN), jnp.float32, -scale(HIDDEN), scale(HIDDEN)), 'W_C': jax.random.uniform(ks[5], (STATE_SIZE, HIDDEN), jnp.float32, -scale(HIDDEN), scale(HIDDEN)), 'D': jax.random.normal(ks[6], (HIDDEN,), dtype=jnp.float32), 'A_log': jnp.log(jnp.tile(jnp.arange(1, STATE_SIZE + 1, dtype=jnp.float32), (HIDDEN, 1)))}
        return inp
    _L1_attn_all = _L1_attn_setup()
    _L1_attn_in = {k: v for k, v in _L1_attn_all.items() if k in ('W_dt_in', 'W_dt_out', 'b_dt_out', 'W_B', 'W_C', 'D', 'A_log')}
    del _L1_attn_all

    def _L1_ffn_setup():
        import jax, jax.numpy as jnp
        import numpy as np
        HIDDEN = 512
        INTER = 1376
        LUT_SIZE = 16

        def _ghost_linear(x, idx, lut):
            w = lut[idx]
            return jnp.einsum('bsh,oh->bso', x, w)
        key = jax.random.key(seed)
        k_x, k_lut, k_g, k_u, k_d = jax.random.split(key, 5)
        x = jax.random.normal(k_x, (2, 1024, HIDDEN), dtype=jnp.float32)
        lut = jax.random.normal(k_lut, (LUT_SIZE,), dtype=jnp.float32) * 0.02
        gate_idx = jax.random.randint(k_g, (INTER, HIDDEN), 0, LUT_SIZE, dtype=jnp.int32)
        up_idx = jax.random.randint(k_u, (INTER, HIDDEN), 0, LUT_SIZE, dtype=jnp.int32)
        down_idx = jax.random.randint(k_d, (HIDDEN, INTER), 0, LUT_SIZE, dtype=jnp.int32)
        return {'x': x, 'lut': lut, 'gate_idx': gate_idx, 'up_idx': up_idx, 'down_idx': down_idx}
    _L1_ffn_all = _L1_ffn_setup()
    _L1_ffn_in = {k: v for k, v in _L1_ffn_all.items() if k in ('lut', 'gate_idx', 'up_idx', 'down_idx')}
    del _L1_ffn_all
    return {'x': x, 'L0_tok_log_dt': _L0_tok_in['log_dt'], 'L0_tok_B_ri': _L0_tok_in['B_ri'], 'L0_tok_inv_A_real': _L0_tok_in['inv_A_real'], 'L0_tok_A_imag': _L0_tok_in['A_imag'], 'L0_attn_wq': _L0_attn_in['wq'], 'L0_attn_bq': _L0_attn_in['bq'], 'L0_attn_wk': _L0_attn_in['wk'], 'L0_attn_bk': _L0_attn_in['bk'], 'L0_attn_wv': _L0_attn_in['wv'], 'L0_attn_bv': _L0_attn_in['bv'], 'L0_attn_wo': _L0_attn_in['wo'], 'L0_attn_bo': _L0_attn_in['bo'], 'L0_ffn_Wr': _L0_ffn_in['Wr'], 'L0_ffn_br': _L0_ffn_in['br'], 'L0_ffn_W1': _L0_ffn_in['W1'], 'L0_ffn_b1': _L0_ffn_in['b1'], 'L0_ffn_W2': _L0_ffn_in['W2'], 'L0_ffn_b2': _L0_ffn_in['b2'], 'L1_attn_W_dt_in': _L1_attn_in['W_dt_in'], 'L1_attn_W_dt_out': _L1_attn_in['W_dt_out'], 'L1_attn_b_dt_out': _L1_attn_in['b_dt_out'], 'L1_attn_W_B': _L1_attn_in['W_B'], 'L1_attn_W_C': _L1_attn_in['W_C'], 'L1_attn_D': _L1_attn_in['D'], 'L1_attn_A_log': _L1_attn_in['A_log'], 'L1_ffn_lut': _L1_ffn_in['lut'], 'L1_ffn_gate_idx': _L1_ffn_in['gate_idx'], 'L1_ffn_up_idx': _L1_ffn_in['up_idx'], 'L1_ffn_down_idx': _L1_ffn_in['down_idx']}

def reference(x, L0_tok_log_dt, L0_tok_B_ri, L0_tok_inv_A_real, L0_tok_A_imag, L0_attn_wq, L0_attn_bq, L0_attn_wk, L0_attn_bk, L0_attn_wv, L0_attn_bv, L0_attn_wo, L0_attn_bo, L0_ffn_Wr, L0_ffn_br, L0_ffn_W1, L0_ffn_b1, L0_ffn_W2, L0_ffn_b2, L1_attn_W_dt_in, L1_attn_W_dt_out, L1_attn_b_dt_out, L1_attn_W_B, L1_attn_W_C, L1_attn_D, L1_attn_A_log, L1_ffn_lut, L1_ffn_gate_idx, L1_ffn_up_idx, L1_ffn_down_idx):
    import jax
    import jax.numpy as jnp

    def _L0_tok_ref(C_ri, log_dt, B_ri, inv_A_real, A_imag, L):
        import jax, jax.numpy as jnp
        import numpy as np
        CH, H, N, N_SSM, SEQ_L = (1, 256, 64, 256, 512)

        def _kernel(C_ri, log_dt, B_ri, inv_A_real, A_imag, L):
            C = C_ri[..., 0] + 1j * C_ri[..., 1]
            B = B_ri[..., 0] + 1j * B_ri[..., 1]
            A = -jnp.exp(inv_A_real) + 1j * A_imag
            rep = log_dt.shape[0] // inv_A_real.shape[0]
            B = jnp.tile(B, (rep, 1))
            A = jnp.tile(A, (rep, 1))
            dt = jnp.exp(log_dt)
            dtA = A * dt[:, None]
            Ct = B[None] * C / (1.0 - dtA / 2) * dt[:, None]
            dA = (1.0 + dtA / 2) / (1.0 - dtA / 2)
            dA_log = jnp.log(dA)
            l = jnp.arange(L, dtype=jnp.float32)
            V = jnp.exp(dA_log[:, :, None] * l)
            K = 2.0 * jnp.einsum('chn,hnl->chl', Ct, V).real
            return K
        return _kernel(C_ri, log_dt, B_ri, inv_A_real, A_imag, L)

    def _L0_attn_ref(x, wq, bq, wk, bk, wv, bv, wo, bo):
        import jax, jax.numpy as jnp
        import numpy as np
        D_MODEL = 512
        NUM_HEADS = 16
        D_K = D_MODEL // NUM_HEADS

        def _heads(t, B, S):
            return t.reshape(B, S, NUM_HEADS, D_K).transpose(0, 2, 1, 3)
        B, S, _ = x.shape
        Q = _heads(x @ wq.T + bq, B, S)
        K = _heads(x @ wk.T + bk, B, S)
        V = _heads(x @ wv.T + bv, B, S)
        Q = jax.nn.elu(Q) + 1.0
        K = jax.nn.elu(K) + 1.0
        KV = jnp.einsum('bhsd,bhse->bhde', K, V)
        QKV = jnp.einsum('bhsd,bhde->bhse', Q, KV)
        K_sum = jnp.sum(K, axis=-2)
        QK_sum = jnp.einsum('bhsd,bhd->bhs', Q, K_sum)
        out = QKV / (QK_sum[..., None] + 1e-08)
        out = out.transpose(0, 2, 1, 3).reshape(B, S, D_MODEL)
        return out @ wo.T + bo

    def _L0_ffn_ref(x, Wr, br, W1, b1, W2, b2):
        import jax, jax.numpy as jnp
        import numpy as np
        B, S, D = (4, 1024, 512)
        DFF = 4 * D
        SKIP = 0.125
        Bs, Ss, Ds = x.shape
        k = max(int(Ss * SKIP), 1)
        logits = (x @ Wr + br)[..., 0]
        weights, idx = jax.lax.top_k(logits, k)
        perm = jnp.argsort(idx, axis=1)
        tokens = jnp.take_along_axis(idx, perm, axis=1)
        fx = jnp.take_along_axis(x, tokens[..., None], axis=1)
        h = jax.nn.gelu(fx @ W1 + b1, approximate=False)
        out_l = h @ W2 + b2
        tw = jax.nn.softmax(weights, axis=1)
        rw = jnp.take_along_axis(tw, perm, axis=1)
        xw = rw[..., None] * out_l
        bidx = jnp.arange(Bs)[:, None]
        return x.at[bidx, tokens].add(xw)

    def _L1_attn_ref(input, W_dt_in, W_dt_out, b_dt_out, W_B, W_C, D, A_log):
        import jax, jax.numpy as jnp
        import numpy as np
        STATE_SIZE = 16
        HIDDEN = 512
        DT_RANK = 64
        BATCH = 2
        SEQ = 512
        A = -jnp.exp(A_log)
        B = jnp.einsum('bsh,nh->bsn', input, W_B)
        C = jnp.einsum('bsh,nh->bsn', input, W_C)
        dt = jnp.einsum('bsh,rh->bsr', input, W_dt_in)
        dt = jnp.einsum('bsr,hr->bsh', dt, W_dt_out) + b_dt_out
        dt = jax.nn.softplus(dt)
        A_disc = jnp.exp(A[None, None] * dt[..., None])
        B_disc = dt[..., None] * B[:, :, None, :]

        def step(x, t):
            a_t, b_t, c_t, u_t = t
            x = a_t * x + b_t * u_t[..., None]
            y = jnp.einsum('bn,bhn->bh', c_t, x) + D * u_t
            return (x, y)
        xs = (jnp.moveaxis(A_disc, 1, 0), jnp.moveaxis(B_disc, 1, 0), jnp.moveaxis(C, 1, 0), jnp.moveaxis(input, 1, 0))
        x0 = jnp.zeros((input.shape[0], D.shape[0], A_log.shape[1]), dtype=input.dtype)
        _, ys = jax.lax.scan(step, x0, xs)
        return jnp.moveaxis(ys, 0, 1)

    def _L1_ffn_ref(x, lut, gate_idx, up_idx, down_idx):
        import jax, jax.numpy as jnp
        import numpy as np
        HIDDEN = 512
        INTER = 1376
        LUT_SIZE = 16

        def _ghost_linear(x, idx, lut):
            w = lut[idx]
            return jnp.einsum('bsh,oh->bso', x, w)
        gate = _ghost_linear(x, gate_idx, lut)
        up = _ghost_linear(x, up_idx, lut)
        h = jax.nn.silu(gate) * up
        return _ghost_linear(h, down_idx, lut)
    h = _L0_tok_ref(x, L0_tok_log_dt, L0_tok_B_ri, L0_tok_inv_A_real, L0_tok_A_imag, 512)
    h = h + _L0_attn_ref(_layernorm(h, axis=-1), L0_attn_wq, L0_attn_bq, L0_attn_wk, L0_attn_bk, L0_attn_wv, L0_attn_bv, L0_attn_wo, L0_attn_bo)
    h = h + _L0_ffn_ref(_layernorm(h, axis=-1), L0_ffn_Wr, L0_ffn_br, L0_ffn_W1, L0_ffn_b1, L0_ffn_W2, L0_ffn_b2)
    h = h + _L1_attn_ref(_layernorm(h, axis=-1), L1_attn_W_dt_in, L1_attn_W_dt_out, L1_attn_b_dt_out, L1_attn_W_B, L1_attn_W_C, L1_attn_D, L1_attn_A_log)
    h = h + _L1_ffn_ref(_layernorm(h, axis=-1), L1_ffn_lut, L1_ffn_gate_idx, L1_ffn_up_idx, L1_ffn_down_idx)
    return h

_drawn_inputs = setup_inputs


def setup_inputs(seed=0):
    import zlib

    import numpy as np

    out = dict(_drawn_inputs(seed))
    spreads = {'L0_ffn_b1': (0.0, 0.8), 'L0_ffn_b2': (0.0, 0.8)}
    factors = {'L0_attn_wq': 5.667,
     'L0_attn_bq': 8.0,
     'L0_attn_bk': 8.0,
     'L0_ffn_Wr': 8.0,
     'L0_ffn_W1': 8.0,
     'L0_ffn_W2': 8.0,
     'L1_attn_b_dt_out': 3.334}
    for name, (base, spread) in spreads.items():
        noise = np.random.default_rng([zlib.crc32(name.encode()), seed]).standard_normal(out[name].shape)
        drawn = base * np.exp(spread * noise) if base else spread * noise
        out[name] = jnp.asarray(drawn.astype(out[name].dtype))
    for name, factor in factors.items():
        out[name] = (out[name] * factor).astype(out[name].dtype)
    return out
```

```python
import numpy as np
import concourse.bass as bass
from concourse import mybir
from contextlib import ExitStack

F32 = mybir.dt.float32
BF16 = mybir.dt.bfloat16
I32 = mybir.dt.int32
ALU = mybir.AluOpType
ACT = mybir.ActivationFunctionType
AX = mybir.AxisListType

P = 128
NB = 16
SEQ = 256
NSTATE = 64
DM = 512
KB = DM // P
T = SEQ // P
HEADS = 16
DK = DM // HEADS
HPB = P // DK
TOPK = SEQ // 8
DFF = 4 * DM
FB = DFF // P
SS = 16
DTR = 64
INTER = 1376
IB = (INTER + P - 1) // P
ILAST = INTER - (IB - 1) * P
NLUT = 16
EPS = 1e-5

HH = SEQ // P
L0 = P
L1 = DM // L0
HC = 32
NCH = P // HC
LC = L1 * NB
GH = 8
NG = HC // GH
NPOW = 9

WG = 0
WU = KB * INTER
WD = 2 * KB * INTER
WCOLS = WD + IB * DM
WSC = WD // FB
WCH = WCOLS // NB


def due(value):
    return not isinstance(value, int) or value > 0


def each_batch(eng, step, first, last):
    with eng.Fori(first // 2, last // 2) as pair:
        for parity in range(2):
            step(pair * 2 + parity, parity, pair)


def s4d_phase(nc, PS, d):
    ctx = ExitStack()
    with ctx:
        sb = lambda name, shape, dt=F32: ctx.enter_context(nc.sbuf_tensor("s4_" + name, shape, dt))
        sem = lambda name: ctx.enter_context(nc.semaphore("s4_" + name))
        raw = sb("raw", [P, 5, P])
        xc = sb("xc", [P, 2, 2, HC, NB])
        mid = sb("mid", [P, 10, P])
        PR = sb("PR", [P, NPOW, P])
        PI = sb("PI", [P, NPOW, P])
        NPI = sb("NPI", [P, NPOW, P])
        G = sb("G", [P, 3, P])
        W = sb("W", [P, 2, 2, HC, L0])
        Q = sb("Q", [P, 2, HC, LC])
        QB = sb("QB", [P, 2, HC, HH, LC])
        tmp = sb("tmp", [P, 2, 2, HC, L0 // 2])
        hts = sb("hts", [P, 2, LC, HH, HC])

        loaded = sem("loaded")
        xc_in = [sem(f"xc_in{p}") for p in range(2)]
        e_done = sem("e_done")
        par = sem("par")
        ones_set = sem("ones_set")
        cm = sem("cm")
        qb_zero = sem("qb_zero")
        qb_ready = sem("qb_ready")
        prod = sem("prod")
        evac = sem("evac")
        stored = [sem(f"stored{p}") for p in range(2)]
        c_used = sem("c_used")

        steps = 2 + 6 * 4 + 4 + 2 * 4
        dt, ea, a, b, om, op, D, rD, t0, t1 = (mid[:, j, :] for j in range(10))
        s = ea
        block = ctx.enter_context(nc.Block())

        @block.sync
        def _(eng):
            for hh in range(HH):
                eng.dma_start(raw[hh * NSTATE:(hh + 1) * NSTATE, 0, :],
                              d["log_dt"][hh * P:(hh + 1) * P].unsqueeze(0).broadcast_to([NSTATE, P])).then_inc(loaded, 16)
            for j, name in enumerate(["inv_A_real", "A_imag", "B_re", "B_im"]):
                eng.dma_start(raw[:, 1 + j, :], d[name]).then_inc(loaded, 16)

            def chunk(i, p, half):
                if due(i - 1):
                    eng.wait_ge(c_used, i - 1)
                for ri in range(2):
                    eng.dma_start(xc[:, p, ri, :, :], d["xc"][:, ri, bass.ds(i * HC, HC), :]).then_inc(xc_in[p], 16)
            chunk(0, 0, 0)
            chunk(1, 1, 0)
            each_batch(eng, chunk, 2, NCH)

        @block.scalar
        def _(eng):
            eng.wait_ge(loaded, 6 * 16)
            eng.activation(dt, raw[:, 0, :], ACT.Exp).then_inc(e_done, 1)
            eng.activation(ea, raw[:, 1, :], ACT.Exp).then_inc(e_done, 1)
            eng.wait_ge(qb_zero, 1)

            def chunk(i, p, half):
                if due(i * NG):
                    eng.wait_ge(prod, i * NG)
                eng.wait_ge(cm, (i + 1) * steps)
                for hh in range(HH):
                    rows = slice(hh * NSTATE, (hh + 1) * NSTATE)
                    eng.activation(QB[rows, :, :, hh, :], Q[rows], ACT.Copy).then_inc(qb_ready, 1)
                if due(half * 16):
                    eng.wait_ge(stored[p], half * 16)
                for g in range(NG):
                    eng.wait_ge(prod, i * NG + g + 1)
                    for r in range(2):
                        last = eng.activation(
                            hts[:, p, :, :, g * GH + r * GH // 2:g * GH + (r + 1) * GH // 2],
                            PS[:, 2 * g + r, :].rearrange("p (h x q) -> p q x h", x=HH, q=LC), ACT.Copy)
                    last.then_inc(evac, 1)
            chunk(0, 0, 0)
            chunk(1, 1, 0)
            each_batch(eng, chunk, 2, NCH)

        @block.gpsimd
        def _(eng):
            eng.memset(QB[:, :, :, :, :], 0.0).then_inc(qb_zero, 1)

            def chunk(i, p, half):
                eng.wait_ge(evac, (i + 1) * NG)
                eng.dma_start(d["hT"][bass.ds(i, 1)], hts[:, p].rearrange("p q a b -> p (q a b)")).then_inc(stored[p], 16)
            for p in range(2):
                chunk(p, p, 0)
            each_batch(eng, chunk, 2, NCH)
            for p in range(2):
                eng.wait_ge(stored[p], NCH // 2 * 16)

        @block.vector
        def _(eng):
            n = 0

            def done(ins):
                nonlocal n
                n += 1
                ins.then_inc(par, 1)
                eng.wait_ge(par, n)

            for p in range(2):
                eng.memset(W[:, p, 0, :, 0:1], 1.0).then_inc(ones_set, 1)
                eng.memset(W[:, p, 1, :, 0:1], 0.0).then_inc(ones_set, 1)
            eng.wait_ge(loaded, 6 * 16)
            eng.wait_ge(e_done, 2)
            done(eng.scalar_tensor_tensor(out=a, in0=ea, scalar=-0.5, in1=dt, op0=ALU.mult, op1=ALU.mult))
            done(eng.scalar_tensor_tensor(out=b, in0=raw[:, 2, :], scalar=0.5, in1=dt, op0=ALU.mult, op1=ALU.mult))
            done(eng.tensor_scalar(om, a, -1.0, 1.0, ALU.mult, ALU.add))
            done(eng.tensor_scalar(op, a, 1.0, None, ALU.add))
            done(eng.tensor_tensor(t0, om, om, ALU.mult))
            done(eng.tensor_tensor(t1, b, b, ALU.mult))
            done(eng.tensor_tensor(D, t0, t1, ALU.add))
            done(eng.reciprocal(rD, D))
            done(eng.tensor_tensor(t0, om, op, ALU.mult))
            done(eng.tensor_tensor(t0, t0, t1, ALU.subtract))
            done(eng.tensor_tensor(PR[:, 0, :], t0, rD, ALU.mult))
            done(eng.scalar_tensor_tensor(out=PI[:, 0, :], in0=b, scalar=2.0, in1=rD, op0=ALU.mult, op1=ALU.mult))
            done(eng.scalar_tensor_tensor(out=s, in0=dt, scalar=2.0, in1=rD, op0=ALU.mult, op1=ALU.mult))
            Br, Bi = raw[:, 3, :], raw[:, 4, :]
            done(eng.tensor_tensor(t0, Br, om, ALU.mult))
            done(eng.tensor_tensor(t1, Bi, b, ALU.mult))
            done(eng.tensor_tensor(t0, t0, t1, ALU.subtract))
            done(eng.tensor_tensor(G[:, 0, :], t0, s, ALU.mult))
            done(eng.tensor_tensor(t0, Br, b, ALU.mult))
            done(eng.tensor_tensor(t1, Bi, om, ALU.mult))
            done(eng.tensor_tensor(t0, t0, t1, ALU.add))
            done(eng.scalar_tensor_tensor(out=G[:, 1, :], in0=t0, scalar=-1.0, in1=s, op0=ALU.mult, op1=ALU.mult))
            done(eng.tensor_scalar(G[:, 2, :], G[:, 0, :], -1.0, None, ALU.mult))
            for k in range(1, NPOW):
                pr, pi = PR[:, k - 1, :], PI[:, k - 1, :]
                done(eng.tensor_tensor(t0, pr, pi, ALU.subtract))
                done(eng.tensor_tensor(t1, pr, pi, ALU.add))
                done(eng.tensor_tensor(PR[:, k, :], t0, t1, ALU.mult))
                done(eng.scalar_tensor_tensor(out=PI[:, k, :], in0=pr, scalar=2.0, in1=pi, op0=ALU.mult, op1=ALU.mult))
            done(eng.tensor_scalar(NPI[:, :, :], PI[:, :, :], -1.0, None, ALU.mult))
            eng.wait_ge(ones_set, 4)

            def power(table, k, i, cols):
                return table[:, k, bass.ds(i * HC, HC)].unsqueeze(2).broadcast_to([P, HC, cols])

            def both(ap, cols):
                return ap.unsqueeze(1).broadcast_to([P, 2, HC, cols])

            def chunk(i, p, half):
                at = 0

                def step(ins):
                    nonlocal at
                    at += 1
                    ins.then_inc(cm, 1)

                def settle():
                    eng.wait_ge(cm, i * steps + at)

                def times(out, src, k, cols, conj):
                    pr = power(PR, k, i, cols)
                    plus, minus = (power(NPI, k, i, cols), power(PI, k, i, cols)) if conj else (power(PI, k, i, cols), power(NPI, k, i, cols))
                    t, v = tmp[:, 0, :, :, 0:cols], tmp[:, 1, :, :, 0:cols]
                    step(eng.tensor_tensor(t, src, both(pr, cols), ALU.mult))
                    step(eng.tensor_tensor(v[:, 0], src[:, 1], minus, ALU.mult))
                    step(eng.tensor_tensor(v[:, 1], src[:, 0], plus, ALU.mult))
                    settle()
                    step(eng.tensor_tensor(out, t, v, ALU.add))
                    settle()

                if due((i - 1) * NG):
                    eng.wait_ge(prod, (i - 1) * NG)
                w, q = W[:, p], Q
                step(eng.tensor_copy(w[:, 0, :, 1:2], PR[:, 0, bass.ds(i * HC, HC)].unsqueeze(2)))
                step(eng.tensor_copy(w[:, 1, :, 1:2], PI[:, 0, bass.ds(i * HC, HC)].unsqueeze(2)))
                settle()
                for k in range(1, 7):
                    m = 2 ** k
                    times(w[:, :, :, m:2 * m], w[:, :, :, 0:m], k, m, False)
                eng.wait_ge(xc_in[p], (half + 1) * 32)
                c = xc[:, p]
                g = lambda j: G[:, j, bass.ds(i * HC, HC)].unsqueeze(2).broadcast_to([P, HC, NB])
                t, v = tmp[:, 0, :, :, 0:NB], tmp[:, 1, :, :, 0:NB]
                if due(i * 2):
                    eng.wait_ge(qb_ready, i * 2)
                step(eng.tensor_tensor(t[:, 0], c[:, 0], g(0), ALU.mult))
                step(eng.tensor_tensor(t[:, 1], c[:, 0], g(1), ALU.mult))
                step(eng.tensor_tensor(v[:, 0], c[:, 1], g(1), ALU.mult))
                step(eng.tensor_tensor(v[:, 1], c[:, 1], g(2), ALU.mult))
                settle()
                eng.tensor_tensor(q[:, :, :, 0:NB], t, v, ALU.add).then_inc(c_used, 1)
                eng.wait_ge(c_used, i + 1)
                times(q[:, :, :, NB:2 * NB], q[:, :, :, 0:NB], 7, NB, True)
                times(q[:, :, :, 2 * NB:4 * NB], q[:, :, :, 0:2 * NB], 8, 2 * NB, True)
                assert at == steps

            for p in range(2):
                chunk(p, p, 0)
            each_batch(eng, chunk, 2, NCH)

        @block.tensor
        def _(eng):
            def chunk(i, p, half):
                eng.wait_ge(qb_ready, (i + 1) * 2)
                for g in range(NG):
                    if due((i - 1) * NG + g + 1):
                        eng.wait_ge(evac, (i - 1) * NG + g + 1)
                    for r in range(GH):
                        bank, at = 2 * g + r // (GH // 2), r % (GH // 2) * HH * LC
                        for ri in range(2):
                            mm = eng.matmul(PS[:, bank, at:at + HH * LC], W[:, p, ri, g * GH + r, :],
                                            QB[:, ri, g * GH + r, :, :], start=(ri == 0), stop=(ri == 1))
                    mm.then_inc(prod, 1)
            for p in range(2):
                chunk(p, p, 0)
            each_batch(eng, chunk, 2, NCH)
F32R = mybir.dt.float32r
VA = P + HPB
LW = WCH // 2


def split_product(eng, out, left, right, start, stop, **kw):
    (lh, ll), (rh, rl) = left, right
    eng.matmul(out, ll, rh, start=start, stop=False, **kw)
    eng.matmul(out, lh, rl, start=False, stop=False, **kw)
    return eng.matmul(out, lh, rh, start=False, stop=stop, **kw)


def inverse_root(eng, wait_value, stats, mv, ve, rs, nm, halves, free, steps, n, out, apart):
    eng.wait_ge(stats, wait_value)
    if due(n):
        eng.wait_ge(free, n)
        eng.sem_inc(apart, 1)
    eng.tensor_scalar(ve, mv[:, :, 1], EPS, None, ALU.add).then_inc(steps, 1)
    eng.wait_ge(steps, n * 3 + 1)
    eng.tensor_tensor(rs, ve, halves[:, 0:T], ALU.pow).then_inc(steps, 1)
    eng.wait_ge(steps, n * 3 + 2)
    eng.tensor_tensor(ve, mv[:, :, 0], rs, ALU.mult).then_inc(steps, 1)
    eng.wait_ge(steps, n * 3 + 3)
    eng.sem_inc(apart, 1)
    eng.tensor_scalar(nm, ve, -1.0, None, ALU.mult).then_inc(out, 1)


def statistics(eng, tiles, st, mv, steps, n, out, apart):
    for t in range(T):
        eng.bn_stats(st[:, t, :], tiles[t]).then_inc(steps, 1)
    eng.wait_ge(steps, (n + 1) * T)
    eng.sem_inc(apart, 1)
    for t in range(T):
        ins = eng.bn_aggr(mv[:, t, :], st[:, t, :])
    ins.then_inc(out, 1)


def attention_phase(nc, PS, d, C):
    ctx = ExitStack()
    with ctx:
        sb = lambda name, shape, dt=F32: ctx.enter_context(nc.sbuf_tensor("at_" + name, shape, dt))
        sem = lambda name: ctx.enter_context(nc.semaphore("at_" + name))
        ident, halves = C["ident"], C["halves"]
        WH = sb("WH", [P, 4, KB, DM], F32R)
        WL = sb("WL", [P, 4, KB, DM], F32R)
        bq = sb("bq", [P, KB])
        bk = sb("bk", [P, DM])
        bv = sb("bv", [P, DM])
        bo = sb("bo", [P, DM])
        wr = sb("wr", [P, DM])
        br = sb("br", [P, 1])
        mask = sb("mask", [P, VA])
        before = sb("before", [P, T, SEQ])
        ones = sb("ones", [P, SEQ])
        slot = sb("slot", [P, TOPK])
        hT = sb("hT", [P, 2, KB, SEQ])
        st1 = sb("st1", [P, T, 6])
        mv1 = sb("mv1", [P, T, 2])
        ve1 = sb("ve1", [P, T])
        rs1 = sb("rs1", [P, T])
        nm1 = sb("nm1", [P, T])
        st2 = sb("st2", [P, T, 6])
        mv2 = sb("mv2", [P, T, 2])
        ve2 = sb("ve2", [P, T])
        rs2 = sb("rs2", [P, T])
        nm2 = sb("nm2", [P, T])
        xn = sb("xn", [P, T, DM])
        xh = sb("xh", [P, KB, SEQ], F32R)
        xl = sb("xl", [P, KB, SEQ], F32R)
        qe = sb("qe", [P, KB, SEQ])
        qr = sb("qr", [P, KB, SEQ])
        q = sb("q", [P, KB, SEQ])
        kx = sb("kx", [P, T, DM])
        ke = sb("ke", [P, T, DM])
        kf = sb("kf", [P, T, DM])
        va = sb("va", [P, T, KB, VA])
        kv = sb("kv", [P, KB, VA])
        den = sb("den", [P, T, HEADS])
        at = sb("at", [P, T, DM])
        ah = sb("ah", [P, KB, SEQ], F32R)
        al = sb("al", [P, KB, SEQ], F32R)
        h1 = sb("h1", [P, 2, T, DM])
        yn = sb("yn", [P, T, DM])
        hb = sb("hb", [P, T, DM])
        junk = sb("junk", [P, DM])
        lg0 = sb("lg0", [P, T])
        lg = sb("lg", [P, T])
        cnt = sb("cnt", [P, 2, T])
        rank = sb("rank", [P, T])
        mx = sb("mx", [P, 1])
        nmx = sb("nmx", [P, 1])
        ex = sb("ex", [P, T])
        es = sb("es", [P, T])
        rz = sb("rz", [P, 1])
        rw = sb("rw", [P, T])
        oh = sb("oh", [P, T, TOPK])
        ow = sb("ow", [P, T, TOPK])
        fx = sb("fx", [P, KB, TOPK])
        pt = sb("pt", [TOPK, SEQ])
        li = sb("li", [P, 2, LW], I32)
        lm = sb("lm", [P, 4, LW], I32)
        lx = sb("lx", [P, 2, NLUT // 2, LW], I32)
        dl = sb("dl", [P, NLUT // 2], I32)
        stage = lx[:, :, :, :].bitcast(F32).rearrange("p a b c -> p (a b c)")[:, 0:2 * KB * DM].rearrange(
            "p (a k n) -> p a k n", a=2, k=KB)

        w_in = [sem(f"w_in{p}") for p in range(2)]
        c_in = sem("c_in")
        w_high = sem("w_high")
        w_low = sem("w_low")
        const_s = sem("const_s")
        h_in = [sem(f"h_in{p}") for p in range(2)]
        st1_s, mv1_r, root1_s, rs1_r = sem("st1_s"), sem("mv1_r"), sem("root1_s"), sem("rs1_r")
        st2_s, mv2_r, root2_s, rs2_r = sem("st2_s"), sem("mv2_r"), sem("root2_s"), sem("rs2_r")
        t_h, xn_r, t_x, x_high, x_low = sem("t_h"), sem("xn_r"), sem("t_x"), sem("x_high"), sem("x_low")
        p_q, p_k, p_v = sem("p_q"), sem("p_k"), sem("p_v")
        q_exp, q_r, k_sum, k_exp, k_s, k_r, v_r = (sem(n) for n in ("q_exp", "q_r", "k_sum", "k_exp", "k_s", "k_r", "v_r"))
        p_kv, kv_r, p_a, a_s, a_r, t_a, a_high, a_low = (
            sem(n) for n in ("p_kv", "kv_r", "p_a", "a_s", "a_r", "t_a", "a_high", "a_low"))
        p_o, h1_r, y_r, hb_r = sem("p_o"), sem("h1_r"), sem("y_r"), sem("hb_r")
        lg_s, lg_r, p_row, r_s, mx_r, oh_r = (sem(n) for n in ("lg_s", "lg_r", "p_row", "r_s", "mx_r", "oh_r"))
        ex_r, es_r, p_g, w_s, ow_r, fx_r, p_t, pt_r = (
            sem(n) for n in ("ex_r", "es_r", "p_g", "w_s", "ow_r", "fx_r", "p_t", "pt_r"))
        s_hb, s_fx, s_pt = sem("s_hb"), sem("s_fx"), sem("s_pt")
        l_in = [sem(f"l_in{p}") for p in range(2)]
        l_out = [sem(f"l_out{p}") for p in range(2)]
        l_used, l_s, l_r = sem("l_used"), sem("l_s"), sem("l_r")

        _, v_apart, g_apart = C["apart"]

        L_STEPS = 13
        WQ, WK, WV, WO = range(4)
        two = lambda b: PS[:, b:b + 2, :]
        SUMS = (0, 6)

        def sums_of(t):
            return PS[:, SUMS[t]:SUMS[t] + 2, 0:2 * VA].rearrange("p b (c v) -> p b c v", c=2)

        def run(eng, step):
            step(0, 0, 0, tail=False)
            step(1, 1, 0)
            each_batch(eng, step, 2, NB - 2)
            step(NB - 2, 0, NB // 2 - 1)
            step(NB - 1, 1, NB // 2 - 1, head=False)

        block = ctx.enter_context(nc.Block())

        @block.sync
        def _(eng):
            hsrc = d["hT"].rearrange("j p (k c x a) -> p k c x j a", k=L1, c=NB, x=HH)

            def load_h(i, p):
                if due(i - 1):
                    eng.wait_ge(p_o, i - 1)
                for hh in range(HH):
                    for k in range(KB):
                        eng.dma_start(hT[:, p, k, hh * P:(hh + 1) * P].rearrange("p (j a) -> p j a", j=NCH),
                                      hsrc[:, k, i, hh]).then_inc(h_in[p], 16)

            def load_index(i, half):
                if due(i * 2 + half - 1):
                    eng.wait_ge(l_used, i * 2 + half - 1)
                eng.dma_start(li[:, half, :], d["idx"][:, bass.ds(i * WCH + half * LW, LW)]).then_inc(l_in[half], 16)

            def store_weights(i, half):
                eng.wait_ge(l_r, i * 2 + half + 1)
                eng.dma_start(d["w"][:, bass.ds(i * WCH + half * LW, LW)], lx[:, half, 0, :]).then_inc(l_out[half], 16)

            for j in range(4):
                if due(j - 1):
                    eng.wait_ge(w_low, j - 1)
                eng.dma_start(stage[:, j % 2], d["w_attn"][j]).then_inc(w_in[j % 2], 16)
                if j == 0:
                    load_h(0, 0)
                if j == 1:
                    eng.dma_start(bq[:, :], d["bq"]).then_inc(c_in, 16)
                    for tile, name in ((bk, "bk"), (bv, "bv"), (bo, "bo"), (wr, "Wr"), (br, "br")):
                        eng.dma_start(tile[:, :], d[name].unsqueeze(0).broadcast_to([P, tile.shape[1]])).then_inc(c_in, 16)
                    load_index(0, 0)
                    load_index(0, 1)

            def step(i, p, pair, head=True, tail=True):
                if head:
                    load_h(i + 1, 1 - p)
                for half in range(2):
                    if head:
                        load_index(i + 1, half)
                    store_weights(i, half)
            run(eng, step)
            for half in range(2):
                eng.wait_ge(l_out[half], NB * 16)

        @block.gpsimd
        def _(eng):
            eng.memset(mask[:, :], 0.0).then_inc(const_s, 1)
            eng.memset(before[:, :, :], 1.0).then_inc(const_s, 1)
            eng.memset(ones[:, :], 1.0).then_inc(const_s, 1)
            eng.iota(slot[:, :], [[1, TOPK]], base=0, channel_multiplier=0,
                     allow_small_or_imprecise_dtypes=True).then_inc(const_s, 1)
            for t in range(T):
                eng.memset(va[:, t, :, P:VA], 1.0).then_inc(const_s, 1)
            eng.wait_ge(const_s, 6)
            for h in range(HPB):
                rows = slice(h * DK, (h + 1) * DK)
                eng.memset(mask[rows, rows], 1.0).then_inc(const_s, 1)
                eng.memset(mask[rows, P + h:P + h + 1], 1.0).then_inc(const_s, 1)
                eng.wait_ge(const_s, 8 + 2 * h)
            eng.affine_select(out=before[:, :, :], in_=before[:, :, :], compare_op=ALU.is_gt, fill=0.0,
                              base=0, pattern=[[P, T], [-1, SEQ]], channel_multiplier=1).then_inc(const_s, 1)

            def root_h(i):
                inverse_root(eng, i + 1, mv1_r, mv1, ve1[:, :], rs1[:, :], nm1[:, :], halves, xn_r, root1_s, i, rs1_r, g_apart)

            def router(i, p):
                inverse_root(eng, i + 1, mv2_r, mv2, ve2[:, :], rs2[:, :], nm2[:, :], halves, y_r, root2_s, i, rs2_r, g_apart)
                eng.wait_ge(y_r, i + 1)
                if due(i * 16):
                    eng.wait_ge(s_hb, i * 16)
                eng.tensor_tensor(hb[:, :, :], h1[:, p], yn[:, :, :], ALU.add).then_inc(hb_r, 1)
                eng.wait_ge(hb_r, i + 1)
                eng.dma_start(d["hb"][i], hb[:, :, :].rearrange("p t d -> p (t d)")).then_inc(s_hb, 16)

            def step(i, p, pair, head=True, tail=True):
                if tail:
                    router(i - 1, 1 - p)
                if head:
                    root_h(i + 1)
            root_h(0)
            run(eng, step)
            router(NB - 1, 1)
            eng.wait_ge(s_hb, NB * 16)

        @block.scalar
        def _(eng):
            def high_of_weight(j):
                eng.wait_ge(w_in[j % 2], (j // 2 + 1) * 16)
                eng.activation(WH[:, j], stage[:, j % 2], ACT.Copy).then_inc(w_high, 1)

            def normalise(i):
                eng.wait_ge(rs1_r, i + 1)
                if due(i):
                    eng.wait_ge(t_x, i)
                for t in range(T):
                    ins = eng.activation(xn[:, t, :], PS[:, 6 + t, :], ACT.Identity, bias=nm1[:, t:t + 1],
                                         scale=rs1[:, t:t + 1])
                ins.then_inc(xn_r, 1)

            def high_of_x(i):
                eng.wait_ge(t_x, i + 1)
                if due(i):
                    eng.wait_ge(p_v, i)
                eng.activation(xh[:, :, :].rearrange("p k s -> p (k s)"), two(4).rearrange("p b s -> p (b s)"), ACT.Copy).then_inc(x_high, 1)

            def router_input(i, p):
                eng.wait_ge(rs2_r, i + 1)
                if due(i):
                    eng.wait_ge(p_g, i)
                if due(i):
                    eng.wait_ge(hb_r, i)
                if due(i):
                    eng.wait_ge(lg_r, i)
                for t in range(T):
                    ins = eng.activation(yn[:, t, :], h1[:, p, t, :], ACT.Identity, bias=nm2[:, t:t + 1],
                                         scale=rs2[:, t:t + 1])
                ins.then_inc(y_r, 1)

            def exponents(i):
                eng.wait_ge(mx_r, i + 1)
                if due(i):
                    eng.wait_ge(es_r, i)
                eng.activation(ex[:, :], lg[:, :], ACT.Exp, bias=nmx[:, 0:1]).then_inc(ex_r, 1)

            def gathered(i):
                eng.wait_ge(p_g, i + 1)
                if due(i * 16):
                    eng.wait_ge(s_fx, i * 16)
                eng.activation(fx[:, :, :].rearrange("p k r -> p (k r)"), PS[:, 3, 0:KB * TOPK], ACT.Copy).then_inc(fx_r, 1)
                eng.wait_ge(fx_r, i + 1)
                eng.dma_start(d["fx"][:, :, bass.ds(i * TOPK, TOPK)], fx[:, :, :]).then_inc(s_fx, 16)

            def spreading(i):
                eng.wait_ge(p_t, i + 1)
                if due(i * 16):
                    eng.wait_ge(s_pt, i * 16)
                eng.activation(pt[:, :], PS[0:TOPK, 2, 0:SEQ], ACT.Copy).then_inc(pt_r, 1)
                eng.wait_ge(pt_r, i + 1)
                eng.dma_start(d["pt"][:, bass.ds(i * SEQ, SEQ)], pt[:, :]).then_inc(s_pt, 16)

            def step(i, p, pair, head=True, tail=True):
                if tail:
                    router_input(i - 1, 1 - p)
                eng.wait_ge(p_q, i + 1)
                if due(i):
                    eng.wait_ge(q_r, i)
                for ob in range(KB):
                    src = PS[:, ob // 2, ob % 2 * SEQ:(ob % 2 + 1) * SEQ]
                    eng.activation(qe[:, ob], src, ACT.Exp, bias=bq[:, ob:ob + 1])
                    ins = eng.activation(qr[:, ob], src, ACT.Relu, bias=bq[:, ob:ob + 1])
                ins.then_inc(q_exp, 1)
                eng.wait_ge(k_sum, i + 1)
                if due(i):
                    eng.wait_ge(k_r, i)
                eng.activation(ke[:, :, :], kx[:, :, :], ACT.Exp).then_inc(k_exp, 1)
                if head:
                    normalise(i + 1)
                if tail:
                    exponents(i - 1)
                if head:
                    high_of_x(i + 1)
                if tail:
                    gathered(i - 1)
                eng.wait_ge(t_a, i + 1)
                if due(i):
                    eng.wait_ge(p_o, i)
                eng.activation(ah[:, :, :].rearrange("p k s -> p (k s)"), two(4).rearrange("p b s -> p (b s)"), ACT.Copy).then_inc(a_high, 1)
                if tail:
                    spreading(i - 1)

            high_of_weight(0)
            high_of_weight(1)
            normalise(0)
            high_of_x(0)
            high_of_weight(2)
            high_of_weight(3)
            eng.wait_ge(c_in, 6 * 16)
            run(eng, step)
            router_input(NB - 1, 1)
            exponents(NB - 1)
            gathered(NB - 1)
            spreading(NB - 1)
            eng.wait_ge(s_fx, NB * 16)
            eng.wait_ge(s_pt, NB * 16)

        @block.vector
        def _(eng):
            lut = C["lut"]
            eng.tensor_tensor(dl[:, :], lut[:, 0:NLUT:2], lut[:, 1:NLUT:2], ALU.bitwise_xor).then_inc(l_s, 1)

            def low_of_weight(j):
                eng.wait_ge(w_high, j + 1)
                eng.tensor_tensor(WL[:, j], stage[:, j % 2], WH[:, j].bitcast(F32), ALU.subtract).then_inc(w_low, 1)

            def bits(i, half):
                base = (i * 2 + half) * L_STEPS + 1
                eng.wait_ge(l_in[half], (i + 1) * 16)
                if due(i * 16):
                    eng.wait_ge(l_out[half], i * 16)
                if due(i * 2 + half):
                    eng.wait_ge(l_r, i * 2 + half)
                x = li[:, half, :]
                eng.tensor_scalar(lm[:, 0], x, 31, 31, ALU.logical_shift_left, ALU.arith_shift_right).then_inc(l_s, 1)
                for b in range(1, 4):
                    ins = eng.tensor_scalar(lm[:, b], x, 1 << b, None, ALU.bitwise_and)
                    ins.then_inc(l_used if b == 3 else l_s, 1)
                eng.wait_ge(l_s, base + 1)
                for j in range(NLUT // 2):
                    eng.tensor_scalar(lx[:, half, j, :], lm[:, 0], dl[:, j:j + 1], lut[:, 2 * j:2 * j + 1],
                                      ALU.bitwise_and, ALU.bitwise_xor).then_inc(l_s, 1)

            def choose(i, half):
                base = (i * 2 + half) * L_STEPS + 1
                eng.wait_ge(l_s, base + 11)
                eng.wait_ge(l_used, i * 2 + half + 1)
                eng.sem_inc(v_apart, 1)
                for b in range(1, 4):
                    n = NLUT >> (b + 1)
                    pairs = lx[:, half].rearrange("p (n two s) c -> p n two s c", two=2, s=1 << (b - 1))
                    ins = eng.copy_predicated(pairs[:, :, 0, 0, :], lm[:, b].unsqueeze(1).broadcast_to([P, n, LW]), pairs[:, :, 1, 0, :])
                    if b < 3:
                        ins.then_inc(l_s, 1)
                        eng.wait_ge(l_s, base + 11 + b)
                        eng.sem_inc(v_apart, 1)
                ins.then_inc(l_r, 1)

            def stats_h(i):
                eng.wait_ge(t_h, i + 1)
                if due(i):
                    eng.wait_ge(rs1_r, i)
                statistics(eng, [PS[:, 6 + t, :] for t in range(T)], st1, mv1, st1_s, i, mv1_r, v_apart)

            def low_of_x(i):
                eng.wait_ge(x_high, i + 1)
                if due(i):
                    eng.wait_ge(p_v, i)
                eng.tensor_tensor(xl[:, :, :].rearrange("p k s -> p (k s)"), two(4).rearrange("p b s -> p (b s)"),
                                  xh[:, :, :].bitcast(F32).rearrange("p k s -> p (k s)"), ALU.subtract).then_inc(x_low, 1)

            def stats_h1(i, p):
                eng.wait_ge(h1_r, i + 1)
                if due(i):
                    eng.wait_ge(rs2_r, i)
                statistics(eng, [h1[:, p, t, :] for t in range(T)], st2, mv2, st2_s, i, mv2_r, v_apart)

            def logits(i):
                eng.wait_ge(y_r, i + 1)
                if due(i):
                    eng.wait_ge(p_row, i)
                if due(i):
                    eng.wait_ge(ex_r, i)
                for t in range(T):
                    eng.scalar_tensor_tensor(out=junk[:, :], in0=yn[:, t, :], scalar=1.0, in1=wr[:, :], op0=ALU.mult,
                                             op1=ALU.mult, accum_out=lg0[:, t:t + 1]).then_inc(lg_s, 1)
                    eng.wait_ge(lg_s, i * T + t + 1)
                eng.tensor_scalar(lg[:, :], lg0[:, :], br[:, 0:1], None, ALU.add).then_inc(lg_r, 1)

            def ranks(i):
                eng.wait_ge(p_row, i + 1)
                eng.wait_ge(lg_r, i + 1)
                if due(i):
                    eng.wait_ge(ow_r, i)
                row = PS[:, 2, 0:SEQ]
                base = i * 6
                for t in range(T):
                    eng.scalar_tensor_tensor(out=junk[:, 0:SEQ], in0=row, scalar=lg[:, t:t + 1], in1=ones[:, :],
                                             op0=ALU.is_gt, op1=ALU.mult, accum_out=cnt[:, 0, t:t + 1]).then_inc(r_s, 1)
                    eng.wait_ge(r_s, base + 2 * t + 1)
                    eng.scalar_tensor_tensor(out=junk[:, 0:SEQ], in0=row, scalar=lg[:, t:t + 1], in1=before[:, t, :],
                                             op0=ALU.is_equal, op1=ALU.mult, accum_out=cnt[:, 1, t:t + 1]).then_inc(r_s, 1)
                    eng.wait_ge(r_s, base + 2 * t + 2)
                eng.tensor_reduce(mx[:, :], row, AX.X, ALU.max).then_inc(r_s, 1)
                eng.tensor_tensor(rank[:, :], cnt[:, 0, :], cnt[:, 1, :], ALU.add).then_inc(r_s, 1)
                eng.wait_ge(r_s, base + 6)
                eng.tensor_scalar(nmx[:, :], mx[:, :], -1.0, None, ALU.mult).then_inc(mx_r, 1)
                if due(i):
                    eng.wait_ge(p_g, i)
                for t in range(T):
                    ins = eng.tensor_scalar(oh[:, t, :], slot[:, :], rank[:, t:t + 1], None, ALU.is_equal)
                ins.then_inc(oh_r, 1)

            def taken(i):
                eng.wait_ge(ex_r, i + 1)
                eng.scalar_tensor_tensor(out=es[:, :], in0=rank[:, :], scalar=float(TOPK), in1=ex[:, :],
                                         op0=ALU.is_lt, op1=ALU.mult).then_inc(es_r, 1)

            def weights(i):
                eng.wait_ge(p_g, i + 1)
                base = i * 2
                eng.reciprocal(rz[:, :], PS[:, 2, SEQ:SEQ + 1]).then_inc(w_s, 1)
                eng.wait_ge(w_s, base + 1)
                eng.tensor_scalar(rw[:, :], es[:, :], rz[:, 0:1], None, ALU.mult).then_inc(w_s, 1)
                eng.wait_ge(w_s, base + 2)
                eng.wait_ge(oh_r, i + 1)
                if due(i):
                    eng.wait_ge(p_t, i)
                for t in range(T):
                    ins = eng.tensor_scalar(ow[:, t, :], oh[:, t, :], rw[:, t:t + 1], None, ALU.mult)
                ins.then_inc(ow_r, 1)

            def step(i, p, pair, head=True, tail=True):
                if tail:
                    stats_h1(i - 1, 1 - p)
                bits(i, 0)
                if tail:
                    logits(i - 1)
                eng.wait_ge(q_exp, i + 1)
                if due(i):
                    eng.wait_ge(p_a, i)
                eng.scalar_tensor_tensor(out=q[:, :, :], in0=qe[:, :, :], scalar=1.0, in1=qr[:, :, :], op0=ALU.min,
                                         op1=ALU.add).then_inc(q_r, 1)
                choose(i, 0)
                eng.wait_ge(p_k, i + 1)
                eng.tensor_tensor(kx[:, :, :], two(2), bk[:, :].unsqueeze(1).broadcast_to([P, T, DM]), ALU.add).then_inc(k_sum, 1)
                eng.wait_ge(k_exp, i + 1)
                eng.tensor_scalar(kx[:, :, :], kx[:, :, :], 0.0, None, ALU.max).then_inc(k_s, 1)
                eng.wait_ge(k_s, i + 1)
                if due(i):
                    eng.wait_ge(p_kv, i)
                eng.scalar_tensor_tensor(out=kf[:, :, :], in0=ke[:, :, :], scalar=1.0, in1=kx[:, :, :], op0=ALU.min,
                                         op1=ALU.add).then_inc(k_r, 1)
                eng.wait_ge(p_v, i + 1)
                for t in range(T):
                    ins = eng.tensor_tensor(va[:, t, :, 0:P], PS[:, 4 + t, :].rearrange("p (b v) -> p b v", b=KB),
                                            bv[:, :].rearrange("p (b v) -> p b v", b=KB), ALU.add)
                ins.then_inc(v_r, 1)
                if head:
                    stats_h(i + 1)
                if tail:
                    ranks(i - 1)
                eng.wait_ge(p_kv, i + 1)
                if due(i):
                    eng.wait_ge(p_a, i)
                eng.tensor_tensor(kv[:, :, :].rearrange("p (b c) v -> p b c v", c=2), sums_of(0),
                                  mask[:, :].unsqueeze(1).unsqueeze(1).broadcast_to([P, 2, 2, VA]), ALU.mult).then_inc(kv_r, 1)
                if tail:
                    taken(i - 1)
                if head:
                    low_of_x(i + 1)
                eng.wait_ge(p_a, i + 1)
                for t in range(T):
                    eng.tensor_scalar(den[:, t, :].rearrange("p (b c h) -> p b c h", b=2, c=2), sums_of(t)[:, :, :, P:VA],
                                      1e-8, None, ALU.add).then_inc(a_s, 1)
                eng.wait_ge(a_s, i * 3 + 2)
                eng.reciprocal(den[:, :, :], den[:, :, :]).then_inc(a_s, 1)
                eng.wait_ge(a_s, i * 3 + 3)
                if due(i):
                    eng.wait_ge(t_a, i)
                for t in range(T):
                    for b in range(2):
                        heads = den[:, t, b * 8:(b + 1) * 8].rearrange("p (c h) -> p c h", c=2)
                        ins = eng.tensor_tensor(
                            at[:, t, b * 2 * P:(b + 1) * 2 * P].rearrange("p (c h e) -> p c h e", c=2, h=HPB),
                            sums_of(t)[:, b, :, 0:P].rearrange("p c (h e) -> p c h e", h=HPB),
                            heads.unsqueeze(3).broadcast_to([P, 2, HPB, DK]), ALU.mult)
                ins.then_inc(a_r, 1)
                if tail:
                    weights(i - 1)
                eng.wait_ge(a_high, i + 1)
                if due(i):
                    eng.wait_ge(p_o, i)
                eng.tensor_tensor(al[:, :, :].rearrange("p k s -> p (k s)"), two(4).rearrange("p b s -> p (b s)"),
                                  ah[:, :, :].bitcast(F32).rearrange("p k s -> p (k s)"), ALU.subtract).then_inc(a_low, 1)
                bits(i, 1)
                choose(i, 1)
                eng.wait_ge(p_o, i + 1)
                if due(i - 1):
                    eng.wait_ge(hb_r, i - 1)
                if due(i - 1):
                    eng.wait_ge(y_r, i - 1)
                eng.tensor_tensor(h1[:, p], two(6), bo[:, :].unsqueeze(1).broadcast_to([P, T, DM]), ALU.add).then_inc(h1_r, 1)

            low_of_weight(0)
            stats_h(0)
            low_of_weight(1)
            low_of_x(0)
            low_of_weight(2)
            low_of_weight(3)
            eng.wait_ge(w_low, 4)
            eng.wait_ge(c_in, 6 * 16)
            eng.wait_ge(const_s, 15)
            run(eng, step)
            stats_h1(NB - 1, 1)
            logits(NB - 1)
            ranks(NB - 1)
            taken(NB - 1)
            weights(NB - 1)

        @block.tensor
        def _(eng):
            def parts(j, k, cols):
                return WH[:, j, k, cols], WL[:, j, k, cols]

            def x_parts(k, cols):
                return xh[:, k, cols], xl[:, k, cols]

            def tokens_of_h(i, p, count):
                eng.wait_ge(h_in[p], count * HH * KB * 16)
                if due(i - 1):
                    eng.wait_ge(h1_r, i - 1)
                for t in range(T):
                    for k in range(KB):
                        ins = eng.transpose(PS[:, 6 + t, k * P:(k + 1) * P], hT[:, p, k, t * P:(t + 1) * P], ident[:, :])
                ins.then_inc(t_h, 1)

            def features(src, out):
                for t in range(T):
                    for k in range(KB):
                        ins = eng.transpose(PS[:, 4 + k // 2, k % 2 * SEQ + t * P:k % 2 * SEQ + (t + 1) * P],
                                            src[:, t, k * P:(k + 1) * P], ident[:, :])
                ins.then_inc(out, 1)

            def rows(i):
                eng.wait_ge(lg_r, i + 1)
                for t in range(T):
                    ins = eng.matmul(PS[:, 2, t * P:(t + 1) * P], lg[:, t:t + 1].broadcast_to([P, P]), ident[:, :],
                                     start=True, stop=True)
                ins.then_inc(p_row, 1)

            def gather(i):
                eng.wait_ge(oh_r, i + 1)
                eng.wait_ge(es_r, i + 1)
                for t in range(T):
                    eng.matmul(PS[:, 2, SEQ:SEQ + 2], es[:, t:t + 1].broadcast_to([P, P]), ones[:, 0:2],
                               start=(t == 0), stop=(t == T - 1))
                for k in range(KB):
                    for t in range(T):
                        ins = eng.matmul(PS[:, 3, k * TOPK:(k + 1) * TOPK], yn[:, t, k * P:(k + 1) * P], oh[:, t, :],
                                         start=(t == 0), stop=(t == T - 1))
                ins.then_inc(p_g, 1)

            def spread(i):
                eng.wait_ge(ow_r, i + 1)
                for t in range(T):
                    ins = eng.transpose(PS[0:TOPK, 2, t * P:(t + 1) * P], ow[:, t, :], ident[:, :])
                ins.then_inc(p_t, 1)

            def step(i, p, pair, head=True, tail=True):
                eng.wait_ge(x_low, i + 1)
                if due(i):
                    eng.wait_ge(a_r, i)
                if not tail:
                    eng.wait_ge(w_low, WQ + 1)
                for ob in range(KB):
                    out = PS[:, ob // 2, ob % 2 * SEQ:(ob % 2 + 1) * SEQ]
                    for k in range(KB):
                        ins = split_product(eng, out, parts(WQ, k, slice(ob * P, (ob + 1) * P)), x_parts(k, slice(0, SEQ)),
                                            k == 0, k == KB - 1)
                ins.then_inc(p_q, 1)
                if due(i - 1):
                    eng.wait_ge(pt_r, i - 1)
                if not tail:
                    eng.wait_ge(w_low, WK + 1)
                for t in range(T):
                    for k in range(KB):
                        ins = split_product(eng, PS[:, 2 + t, :], x_parts(k, slice(t * P, (t + 1) * P)),
                                            parts(WK, k, slice(0, DM)), k == 0, k == KB - 1)
                ins.then_inc(p_k, 1)
                if due(i):
                    eng.wait_ge(a_low, i)
                if not tail:
                    eng.wait_ge(w_low, WV + 1)
                for t in range(T):
                    for k in range(KB):
                        ins = split_product(eng, PS[:, 4 + t, :], x_parts(k, slice(t * P, (t + 1) * P)),
                                            parts(WV, k, slice(0, DM)), k == 0, k == KB - 1)
                ins.then_inc(p_v, 1)
                if head:
                    tokens_of_h(i + 1, 1 - p, pair + 1 + p)
                eng.wait_ge(k_sum, i + 1)
                if tail:
                    rows(i - 1)
                eng.wait_ge(q_exp, i + 1)
                eng.wait_ge(k_r, i + 1)
                eng.wait_ge(v_r, i + 1)
                for b in range(KB):
                    for t in range(T):
                        ins = eng.matmul(sums_of(0)[:, b // 2, b % 2, :], kf[:, t, b * P:(b + 1) * P], va[:, t, b, :],
                                         start=(t == 0), stop=(t == T - 1))
                ins.then_inc(p_kv, 1)
                if head:
                    eng.wait_ge(xn_r, i + 2)
                    features(xn, t_x)
                eng.wait_ge(q_r, i + 1)
                eng.wait_ge(kv_r, i + 1)
                if not head:
                    if due(i):
                        eng.wait_ge(h1_r, i)
                for t in range(T):
                    for b in range(KB):
                        ins = eng.matmul(sums_of(t)[:, b // 2, b % 2, :], q[:, b, t * P:(t + 1) * P], kv[:, b, :],
                                         start=True, stop=True)
                ins.then_inc(p_a, 1)
                if tail:
                    gather(i - 1)
                if head:
                    eng.wait_ge(x_low, i + 2)
                eng.wait_ge(a_r, i + 1)
                features(at, t_a)
                if tail:
                    spread(i - 1)
                eng.wait_ge(a_low, i + 1)
                if not tail:
                    eng.wait_ge(w_low, WO + 1)
                for t in range(T):
                    for k in range(KB):
                        split_product(eng, PS[:, 6 + t, :], (ah[:, k, t * P:(t + 1) * P], al[:, k, t * P:(t + 1) * P]),
                                      parts(WO, k, slice(0, DM)), k == 0, False, skip_group_check=True)
                    for k in range(KB):
                        ins = eng.matmul(PS[:, 6 + t, k * P:(k + 1) * P], hT[:, p, k, t * P:(t + 1) * P], ident[:, :],
                                         start=False, stop=True, is_transpose=True, skip_group_check=True)
                ins.then_inc(p_o, 1)

            tokens_of_h(0, 0, 1)
            eng.wait_ge(xn_r, 1)
            features(xn, t_x)
            run(eng, step)
            eng.wait_ge(k_sum, NB)
            rows(NB - 1)
            gather(NB - 1)
            spread(NB - 1)


def routed_ffn_phase(nc, PS, d, C):
    ctx = ExitStack()
    with ctx:
        sb = lambda name, shape, dt=F32: ctx.enter_context(nc.sbuf_tensor("ff_" + name, shape, dt))
        sem = lambda name: ctx.enter_context(nc.semaphore("ff_" + name))
        NT = NB * TOPK
        fx = sb("fx", [P, KB, NT])
        fh = sb("fh", [P, KB, NT], F32R)
        fl = sb("fl", [P, KB, NT], F32R)
        b1 = sb("b1", [P, FB])
        b2 = sb("b2", [P, DM])
        w1 = sb("w1", [P, 2, KB, P])
        w1h = sb("w1h", [P, 2, KB, P], F32R)
        w1l = sb("w1l", [P, 2, KB, P], F32R)
        w2 = sb("w2", [P, 2, DM])
        w2h = sb("w2h", [P, 2, DM], F32R)
        w2l = sb("w2l", [P, 2, DM], F32R)
        g = sb("g", [P, 2, NT])
        gh = sb("gh", [P, 2, NT], F32R)
        gl = sb("gl", [P, 2, NT], F32R)
        ol = sb("ol", [P, NT // P, DM])
        ws = sb("ws", [P, 2, WSC])

        c_in = sem("c_in")
        down_in = sem("down_in")
        ws_in = [sem(f"ws_in{p}") for p in range(2)]
        ws_high, ws_low = sem("ws_high"), sem("ws_low")
        w1_in = [sem(f"w1_in{p}") for p in range(2)]
        w2_in = [sem(f"w2_in{p}") for p in range(2)]
        x_high, x_low = sem("x_high"), sem("x_low")
        w1_high, w1_low, w2_high, w2_low = sem("w1_high"), sem("w1_low"), sem("w2_high"), sem("w2_low")
        p_1 = sem("p_1")
        p_2 = sem("p_2")
        g_r, g_high, g_low = sem("g_r"), sem("g_high"), sem("g_low")
        o_r, o_out = sem("o_r"), sem("o_out")
        a_apart, v_apart, _ = C["apart"]

        block = ctx.enter_context(nc.Block())

        def run(eng, step):
            step(0, 0, 0)
            step(1, 1, 0)
            each_batch(eng, step, 2, FB)

        @block.sync
        def _(eng):
            eng.dma_start(fx[:, :, :], d["fx"]).then_inc(c_in, 16)
            eng.dma_start(b1[:, :], d["b1"]).then_inc(c_in, 16)
            eng.dma_start(b2[:, :], d["b2"].unsqueeze(0).broadcast_to([P, DM])).then_inc(c_in, 16)

            def step(f, p, pair):
                if due(f - 1):
                    eng.wait_ge(w1_low, f - 1)
                if due(f - 1):
                    eng.wait_ge(w2_low, f - 1)
                eng.dma_start(w1[:, p], d["W1"][f]).then_inc(w1_in[p], 16)
                eng.dma_start(w2[:, p], d["W2"][f]).then_inc(w2_in[p], 16)
            run(eng, step)
            eng.wait_ge(o_r, NT // P)
            eng.dma_start(d["ol"].rearrange("(g p) d -> p g d", p=P), ol[:, :, :]).then_inc(o_out, 16)
            eng.wait_ge(o_out, 16)

        @block.gpsimd
        def _(eng):
            def step(f, p, pair):
                if due(f - 1):
                    eng.wait_ge(ws_low, f - 1)
                eng.dma_start(ws[:, p], d["w"][:, bass.ds(f * WSC, WSC)].bitcast(F32)).then_inc(ws_in[p], 16)
            run(eng, step)
            eng.dma_start(C["wd"][:, :], d["w"][:, WD:WCOLS].bitcast(F32)).then_inc(down_in, 16)
            eng.wait_ge(down_in, 16)

        @block.scalar
        def _(eng):
            eng.wait_ge(c_in, 3 * 16)
            eng.activation(fh[:, :, :], fx[:, :, :], ACT.Copy).then_inc(x_high, 1)

            def step(f, p, pair):
                eng.wait_ge(w1_in[p], (pair + 1) * 16)
                if due(f - 1):
                    eng.wait_ge(p_1, f - 1)
                eng.activation(w1h[:, p], w1[:, p], ACT.Copy).then_inc(w1_high, 1)
                eng.wait_ge(w2_in[p], (pair + 1) * 16)
                if due(f - 1):
                    eng.wait_ge(p_2, f - 1)
                eng.activation(w2h[:, p], w2[:, p], ACT.Copy).then_inc(w2_high, 1)
                if due(f - 1):
                    eng.wait_ge(g_low, f - 1)
                eng.wait_ge(p_1, f + 1)
                eng.sem_inc(a_apart, 1)
                eng.activation(g[:, p, :], PS[:, 4 + p, :], ACT.Gelu, bias=b1[:, bass.ds(f, 1)]).then_inc(g_r, 1)
                eng.wait_ge(g_r, f + 1)
                eng.activation(gh[:, p, :], g[:, p, :], ACT.Copy).then_inc(g_high, 1)
                eng.wait_ge(ws_in[p], (pair + 1) * 16)
                eng.sem_inc(a_apart, 1)
                eng.activation(C["wgh"][:, bass.ds(f * WSC, WSC)], ws[:, p], ACT.Copy).then_inc(ws_high, 1)
            run(eng, step)

        @block.vector
        def _(eng):
            eng.wait_ge(x_high, 1)
            eng.tensor_tensor(fl[:, :, :], fx[:, :, :], fh[:, :, :].bitcast(F32), ALU.subtract).then_inc(x_low, 1)

            def step(f, p, pair):
                eng.wait_ge(w1_high, f + 1)
                eng.tensor_tensor(w1l[:, p], w1[:, p], w1h[:, p].bitcast(F32), ALU.subtract).then_inc(w1_low, 1)
                eng.wait_ge(w2_high, f + 1)
                eng.tensor_tensor(w2l[:, p], w2[:, p], w2h[:, p].bitcast(F32), ALU.subtract).then_inc(w2_low, 1)
                eng.wait_ge(g_high, f + 1)
                eng.tensor_tensor(gl[:, p, :], g[:, p, :], gh[:, p, :].bitcast(F32), ALU.subtract).then_inc(g_low, 1)
                eng.wait_ge(ws_high, f + 1)
                eng.sem_inc(v_apart, 1)
                eng.tensor_tensor(C["wgl"][:, bass.ds(f * WSC, WSC)], ws[:, p],
                                  C["wgh"][:, bass.ds(f * WSC, WSC)].bitcast(F32), ALU.subtract).then_inc(ws_low, 1)
            run(eng, step)
            eng.wait_ge(p_2, FB)
            eng.wait_ge(c_in, 3 * 16)
            for t in range(NT // P):
                eng.tensor_tensor(ol[:, t, :], PS[:, t, :], b2[:, :], ALU.add).then_inc(o_r, 1)

        @block.tensor
        def _(eng):
            def first(f, p):
                eng.wait_ge(w1_low, f + 1)
                if due(f - 1):
                    eng.wait_ge(g_r, f - 1)
                for k in range(KB):
                    ins = split_product(eng, PS[:, 4 + p, :], (w1h[:, p, k, :], w1l[:, p, k, :]), (fh[:, k, :], fl[:, k, :]),
                                        k == 0, k == KB - 1)
                ins.then_inc(p_1, 1)

            def second(f, p, start=False, stop=False):
                eng.wait_ge(w2_low, f + 1)
                eng.wait_ge(g_low, f + 1)
                for t in range(NT // P):
                    cols = slice(t * P, (t + 1) * P)
                    ins = split_product(eng, PS[:, t, :], (gh[:, p, cols], gl[:, p, cols]), (w2h[:, p, :], w2l[:, p, :]), start, stop)
                ins.then_inc(p_2, 1)

            def step(f, p, pair):
                first(f, p)
                second(f - 1, 1 - p)
            eng.wait_ge(x_low, 1)
            first(0, 0)
            first(1, 1)
            second(0, 0, start=True)
            each_batch(eng, step, 2, FB)
            second(FB - 1, (FB - 1) % 2, stop=True)


def scan_phase(nc, PS, d, C):
    ctx = ExitStack()
    with ctx:
        sb = lambda name, shape, dt=F32: ctx.enter_context(nc.sbuf_tensor("sc_" + name, shape, dt))
        sem = lambda name: ctx.enter_context(nc.semaphore("sc_" + name))
        ident, halves, wgh, wgl, wd = C["ident"], C["halves"], C["wgh"], C["wgl"], C["wd"]
        BCR = 2 * SS
        sel = sb("sel", [3 * BCR, BCR], BF16)
        wp = sb("wp", [P, KB, DTR + 3 * BCR])
        right = sb("right", [DTR + TOPK, DM])
        wdo = right[0:DTR]
        ol = right[DTR:DTR + TOPK]
        left = sb("left", [DTR + TOPK, SEQ])
        dtr = left[0:DTR]
        pt = left[DTR:DTR + TOPK]
        bdt = sb("bdt", [P, KB])
        Dc = sb("Dc", [P, KB])
        al = sb("al", [P, KB, SS])
        A = sb("A", [P, KB, SS])
        h2 = sb("h2", [P, 2, T, DM])
        stz = sb("stz", [P, T, 6])
        mvz = sb("mvz", [P, T, 2])
        vez = sb("vez", [P, T])
        rsz = sb("rsz", [P, T])
        nmz = sb("nmz", [P, T])
        xn = sb("xn", [P, T, DM])
        zT = sb("zT", [P, KB, SEQ])
        diag = sb("diag", [P, KB, P])
        b1 = sb("b1", [3 * BCR, SEQ])
        bc = sb("bc", [3 * BCR, 2, SEQ], BF16)
        dt = sb("dt", [P, 2, KB, SEQ])
        du = sb("du", [P, 2, KB, SEQ])
        bs = sb("bs", [P, 2, SEQ])
        a = sb("a", [P, 2, KB, SEQ])
        bu = sb("bu", [P, 2, KB, SEQ])
        cx = sb("cx", [P, 2, KB, SEQ])
        h3 = sb("h3", [P, 2, T, DM])
        stf = sb("stf", [P, T, 6])
        mvf = sb("mvf", [P, T, 2])
        vef = sb("vef", [P, T])
        rsf = sb("rsf", [P, T])
        nmf = sb("nmf", [P, T])
        fh = sb("fh", [P, KB, SEQ], F32R)
        fl = sb("fl", [P, KB, SEQ], F32R)
        th = sb("th", [P, 2, SEQ])
        hh = sb("hh", [P, IB, SEQ])

        c_in, c_s, c_a = sem("c_in"), sem("c_s"), sem("c_a")
        f_in = sem("f_in")
        p_sc, h2_r, stz_s, mvz_r, rootz_s, rsz_r, zn_r, t_z, z_r = (
            sem(n) for n in ("p_sc", "h2_r", "stz_s", "mvz_r", "rootz_s", "rsz_r", "zn_r", "t_z", "z_r"))
        p_pj, dtr_r, bc_s, bc_r, p_dt, xb_r, sp_s, sp_r, dt_s, du_r, dt_r = (
            sem(n) for n in ("p_pj", "dtr_r", "bc_s", "bc_r", "p_dt", "xb_r", "sp_s", "sp_r", "dt_s", "du_r", "dt_r"))
        b_r, p_bc, a_r, bu_s, scan_s, cx_s, p_zd, y_s = (sem(n) for n in ("b_r", "p_bc", "a_r", "bu_s", "scan_s", "cx_s", "p_zd", "y_s"))
        h3_r, stf_s, mvf_r, rootf_s, rsf_r, fn_r, t_f, f_h, f_r = (
            sem(n) for n in ("h3_r", "stf_s", "mvf_r", "rootf_s", "rsf_r", "fn_r", "t_f", "f_h", "f_r"))
        p_gu, th_r, m_s, hh_r, p_dn, h4_r, s_out = (sem(n) for n in ("p_gu", "th_r", "m_s", "hh_r", "p_dn", "h4_r", "s_out"))
        _, v_apart, g_apart = C["apart"]

        YB, MB, CB, GB = 0, 2, 4, 6
        two = lambda b: PS[:, b:b + 2, :]
        rows_of = lambda k: P if k < IB - 1 else ILAST
        DOWN = {15: (0, 1), 0: (2, 3), 1: (4, 5), 2: (6, 7, 8), 3: (9, 10)}
        flat = lambda x: x.rearrange("p k s -> p (k s)")
        by_tile = lambda x: x[:, :, :].rearrange("p k (t s) -> p t k s", t=T)
        by_tile_of = lambda b: PS[:, b:b + T, :].rearrange("p t (k s) -> p t k s", k=KB)

        def run(eng, step):
            step(0, 0, 0, back=False, down=False)
            step(1, 1, 0, down=False)
            step(2, 0, 1)
            step(3, 1, 1)
            each_batch(eng, step, 4, NB - 2)
            step(NB - 2, 0, NB // 2 - 1)
            step(NB - 1, 1, NB // 2 - 1, front=False)
            step(NB, 0, NB // 2, front=False, mid=False)
            step(NB + 1, 1, NB // 2, front=False, mid=False, back=False)

        block = ctx.enter_context(nc.Block())

        @block.sync
        def _(eng):
            eng.dma_start(wp[:, :, 0:DTR], d["w_dti"]).then_inc(c_in, 16)
            for g in range(3):
                at = DTR + g * BCR
                eng.dma_start(wp[:, :, at:at + BCR], d["w_bc"]).then_inc(c_in, 16)
            eng.dma_start(wdo[:, :], d["w_dto"]).then_inc(c_in, 16)
            for tile, name in ((bdt, "b_dt"), (Dc, "D"), ):
                eng.dma_start(tile[:, :], d[name]).then_inc(c_in, 16)
            eng.dma_start(al[:, :, :], d["A_log"]).then_inc(c_in, 16)

            def load(b, p):
                if due(b):
                    eng.wait_ge(h2_r, b)
                if due(b - 1):
                    eng.wait_ge(h3_r, b - 1)
                eng.dma_start(h2[:, p].rearrange("p t d -> p (t d)"), d["hb"][b]).then_inc(f_in, 16)
                eng.dma_start(ol[:, :], d["ol"][bass.ds(b * TOPK, TOPK), :]).then_inc(f_in, 16)
                eng.dma_start(pt[:, :], d["pt"][:, bass.ds(b * SEQ, SEQ)]).then_inc(f_in, 16)

            def store(b, p):
                eng.wait_ge(h4_r, b + 1)
                eng.dma_start(d["out"].rearrange("b (t p) d -> b p t d", p=P)[b], h3[:, p]).then_inc(s_out, 16)

            def step(i, p, pair, front=True, mid=True, back=True, down=True):
                if front:
                    load(i + 1, 1 - p)
                if down:
                    store(i - 2, p)
            load(0, 0)
            run(eng, step)
            eng.wait_ge(s_out, NB * 16)

        @block.gpsimd
        def _(eng):
            eng.memset(sel[:, :], 0.0).then_inc(c_s, 1)
            for g in range(3):
                eng.wait_ge(c_s, g + 1)
                eng.affine_select(out=sel[:, :], in_=sel[:, :], compare_op=ALU.not_equal, fill=1.0,
                                  base=-g * BCR, pattern=[[-1, BCR]], channel_multiplier=1).then_inc(c_s, 1)

            def root_z(b):
                inverse_root(eng, b + 1, mvz_r, mvz, vez[:, :], rsz[:, :], nmz[:, :], halves, zn_r, rootz_s, b, rsz_r, g_apart)

            def root_f(b):
                inverse_root(eng, b + 1, mvf_r, mvf, vef[:, :], rsf[:, :], nmf[:, :], halves, fn_r, rootf_s, b, rsf_r, g_apart)

            def inputs(b, p, n):
                m = b * SS + n
                eng.wait_ge(du_r, b + 1)
                eng.wait_ge(b_r, m + 1)
                if due(m - 1):
                    eng.wait_ge(cx_s, m - 1)
                eng.tensor_tensor(bu[:, n % 2], du[:, p], bs[:, n % 2, :].unsqueeze(1).broadcast_to([P, KB, SEQ]),
                                  ALU.mult).then_inc(bu_s, 1)

            def step(i, p, pair, front=True, mid=True, back=True, down=True):
                for n in range(SS):
                    if back and n == 1:
                        root_f(i - 1)
                    if front and n == 6:
                        root_z(i + 1)
                    if mid and n + 1 < SS:
                        inputs(i, p, n + 1)
                    if front and n + 1 == SS:
                        inputs(i + 1, 1 - p, 0)
            root_z(0)
            inputs(0, 0, 0)
            run(eng, step)

        @block.scalar
        def _(eng):
            eng.wait_ge(c_in, 8 * 16)
            eng.activation(A[:, :, :], al[:, :, :], ACT.Exp).then_inc(c_a, 1)
            eng.wait_ge(c_a, 2)

            def normalise_z(b, p):
                eng.wait_ge(rsz_r, b + 1)
                if due(b - 1):
                    eng.wait_ge(t_f, b - 1)
                for t in range(T):
                    ins = eng.activation(xn[:, t, :], h2[:, p, t, :], ACT.Identity, bias=nmz[:, t:t + 1], scale=rsz[:, t:t + 1])
                ins.then_inc(zn_r, 1)

            def transposed_z(b):
                eng.wait_ge(t_z, b + 1)
                if due(b):
                    eng.wait_ge(p_pj, b)
                if due(b):
                    eng.wait_ge(du_r, b)
                if due(b):
                    eng.wait_ge(p_zd, b)
                for t in range(T):
                    ins = eng.activation(zT[:, :, t * P:(t + 1) * P], PS[:, MB + t, :].rearrange("p (k s) -> p k s", k=KB), ACT.Copy)
                ins.then_inc(z_r, 1)

            def rank_input(b):
                eng.wait_ge(p_pj, b + 1)
                if due(b):
                    eng.wait_ge(p_dt, b)
                eng.activation(dtr[:, :], PS[0:DTR, MB, 0:SEQ], ACT.Copy).then_inc(dtr_r, 1)

            def softplus(b, p):
                eng.wait_ge(xb_r, b + 1)
                if due((b - 1) * SS):
                    eng.wait_ge(a_r, (b - 1) * SS)
                eng.activation(flat(dt[:, p]), flat(du[:, p]), ACT.Abs).then_inc(sp_s, 1)
                eng.wait_ge(sp_s, b * 2 + 1)
                eng.activation(flat(dt[:, p]), flat(dt[:, p]), ACT.Exp, scale=-1.0).then_inc(sp_s, 1)
                eng.wait_ge(sp_s, b * 2 + 2)
                eng.activation(flat(dt[:, p]), flat(dt[:, p]), ACT.Ln, bias=1.0).then_inc(sp_r, 1)

            def everywhere(b, n):
                m = b * SS + n
                eng.wait_ge(p_bc, m + 1)
                if due(m - 1):
                    eng.wait_ge(bu_s, m - 1)
                eng.activation(bs[:, n % 2, :], PS[:, CB + n % 2, 0:SEQ], ACT.Copy).then_inc(b_r, 1)

            def decay(b, p, n):
                m = b * SS + n
                eng.wait_ge(dt_r, b + 1)
                if due(m - 1):
                    eng.wait_ge(scan_s, m - 1)
                for k in range(KB):
                    ins = eng.activation(a[:, n % 2, k, :], dt[:, p, k, :], ACT.Exp, scale=A[:, k, n:n + 1])
                ins.then_inc(a_r, 1)

            def normalise_f(b, p):
                eng.wait_ge(rsf_r, b + 1)
                eng.wait_ge(t_z, min(b + 2, NB) if isinstance(b, int) else b + 2)
                for t in range(T):
                    ins = eng.activation(xn[:, t, :], h3[:, p, t, :], ACT.Identity, bias=nmf[:, t:t + 1], scale=rsf[:, t:t + 1])
                ins.then_inc(fn_r, 1)

            def transposed_f(b):
                eng.wait_ge(t_f, b + 1)
                if due(b * IB):
                    eng.wait_ge(p_gu, b * IB)
                eng.activation(by_tile(fh), by_tile_of(MB), ACT.Copy).then_inc(f_h, 1)

            def tanh(b, k):
                m = rows_of(k)
                eng.wait_ge(p_gu, b * IB + k + 1)
                if due(b * IB + k - (1 if k else 0)):
                    eng.wait_ge(hh_r, b * IB + k - (1 if k else 0))
                eng.activation(th[0:m, k % 2, :], PS[0:m, GB + k % 2, 0:SEQ], ACT.Tanh, scale=0.5).then_inc(th_r, 1)

            def step(i, p, pair, front=True, mid=True, back=True, down=True):
                for n in range(SS):
                    if mid and n + 1 < SS:
                        everywhere(i, n + 1)
                        decay(i, p, n + 1)
                    if front and n + 1 == SS:
                        everywhere(i + 1, 0)
                        decay(i + 1, 1 - p, 0)
                    if back and n == 1:
                        normalise_f(i - 1, 1 - p)
                    if back and n == 2:
                        transposed_f(i - 1)
                    if back and 4 <= n < 4 + IB:
                        tanh(i - 1, n - 4)
                    if front and n == 6:
                        normalise_z(i + 1, 1 - p)
                    if front and n == 7:
                        transposed_z(i + 1)
                    if front and n == 9:
                        rank_input(i + 1)
                    if front and n == 11:
                        softplus(i + 1, 1 - p)

            normalise_z(0, 0)
            transposed_z(0)
            rank_input(0)
            softplus(0, 0)
            everywhere(0, 0)
            decay(0, 0, 0)
            run(eng, step)

        @block.vector
        def _(eng):
            eng.wait_ge(c_in, 8 * 16)
            eng.wait_ge(c_a, 1)
            eng.tensor_scalar(A[:, :, :], A[:, :, :], -1.0, None, ALU.mult).then_inc(c_a, 1)
            for k in range(KB):
                ins = eng.tensor_scalar(diag[:, k, :], ident[:, :], Dc[:, k:k + 1], None, ALU.mult)
            ins.then_inc(c_a, 1)

            def residual_z(b, p):
                eng.wait_ge(p_sc, b + 1)
                eng.tensor_tensor(h2[:, p], two(MB), h2[:, p], ALU.add).then_inc(h2_r, 1)
                eng.wait_ge(h2_r, b + 1)
                if due(b):
                    eng.wait_ge(rsz_r, b)
                statistics(eng, [h2[:, p, t, :] for t in range(T)], stz, mvz, stz_s, b, mvz_r, v_apart)

            def parts(b, p):
                eng.wait_ge(p_pj, b + 1)
                if due((b - 1) * SS):
                    eng.wait_ge(p_bc, (b - 1) * SS)
                if due(b):
                    eng.wait_ge(bc_r, b)
                src = PS[0:3 * BCR, MB + 1, 0:SEQ]
                r = [slice(g * BCR, (g + 1) * BCR) for g in range(3)]
                eng.tensor_copy(bc[:, p, :], src).then_inc(bc_s, 1)
                eng.wait_ge(bc_s, b * 4 + 1)
                eng.tensor_tensor(b1[:, :], src, bc[:, p, :], ALU.subtract).then_inc(bc_s, 1)
                eng.wait_ge(bc_s, b * 4 + 2)
                eng.tensor_copy(bc[r[1], p, :], b1[r[1], :]).then_inc(bc_s, 1)
                eng.tensor_copy(bc[r[2], p, :], b1[r[2], :]).then_inc(bc_s, 1)
                eng.wait_ge(bc_s, b * 4 + 4)
                eng.tensor_tensor(bc[r[2], p, :], b1[r[2], :], bc[r[2], p, :], ALU.subtract).then_inc(bc_r, 1)

            def raw_dt(b, p):
                eng.wait_ge(p_dt, b + 1)
                if due((b - 1) * SS):
                    eng.wait_ge(bu_s, (b - 1) * SS)
                eng.tensor_tensor(du[:, p].rearrange("p (b c) s -> p b c s", c=2), two(MB).rearrange("p b (c s) -> p b c s", c=2),
                                  bdt[:, :].rearrange("p (b c) -> p b c", c=2).unsqueeze(3).broadcast_to([P, 2, 2, SEQ]),
                                  ALU.add).then_inc(xb_r, 1)

            def make_dt(b, p):
                eng.wait_ge(sp_r, b + 1)
                eng.scalar_tensor_tensor(out=flat(dt[:, p]), in0=flat(du[:, p]), scalar=0.0, in1=flat(dt[:, p]),
                                         op0=ALU.max, op1=ALU.add).then_inc(dt_s, 1)

            def make_du(b, p):
                eng.wait_ge(dt_s, b + 1)
                eng.tensor_tensor(flat(du[:, p]), flat(dt[:, p]), flat(zT[:, :, :]), ALU.mult).then_inc(du_r, 1)
                eng.wait_ge(du_r, b + 1)
                eng.memset(dt[:, p, :, 0:1], 1e30).then_inc(dt_r, 1)

            def scan(b, n):
                m = b * SS + n
                eng.wait_ge(a_r, m + 1)
                eng.wait_ge(bu_s, m + 1)
                if due(m):
                    eng.wait_ge(cx_s, m)
                eng.tensor_tensor_scan(flat(bu[:, n % 2]), flat(a[:, n % 2]), flat(bu[:, n % 2]), 0.0, ALU.mult, ALU.add).then_inc(scan_s, 1)

            def outputs(b, n):
                m = b * SS + n
                eng.wait_ge(scan_s, m + 1)
                if due(m - 1):
                    eng.wait_ge(y_s, m - 1)
                eng.tensor_tensor(cx[:, n % 2], bu[:, n % 2], PS[:, CB + n % 2, SEQ:2 * SEQ].unsqueeze(1).broadcast_to([P, KB, SEQ]),
                                  ALU.mult).then_inc(cx_s, 1)

            def residual_f(b, p):
                eng.wait_ge(y_s, (b + 1) * SS)
                if due((b - 1) * 16):
                    eng.wait_ge(s_out, (b - 1) * 16)
                eng.tensor_tensor(h3[:, p], two(YB), h2[:, p], ALU.add).then_inc(h3_r, 1)
                eng.wait_ge(h3_r, b + 1)
                if due(b):
                    eng.wait_ge(rsf_r, b)
                statistics(eng, [h3[:, p, t, :] for t in range(T)], stf, mvf, stf_s, b, mvf_r, v_apart)

            def low_f(b):
                eng.wait_ge(f_h, b + 1)
                if due(b * IB):
                    eng.wait_ge(p_gu, b * IB)
                eng.tensor_tensor(by_tile(fl), by_tile_of(MB), by_tile(fh).bitcast(F32), ALU.subtract).then_inc(f_r, 1)

            def gated(b, k):
                m, at = rows_of(k), b * IB + k
                eng.wait_ge(th_r, at + 1)
                if due(at):
                    eng.wait_ge(hh_r, at)
                eng.scalar_tensor_tensor(out=th[0:m, k % 2, :], in0=th[0:m, k % 2, :], scalar=1.0, in1=PS[0:m, GB + k % 2, 0:SEQ],
                                         op0=ALU.add, op1=ALU.mult).then_inc(m_s, 1)
                eng.wait_ge(m_s, at + 1)
                if due(b):
                    eng.wait_ge(p_dn, b)
                eng.scalar_tensor_tensor(out=hh[0:m, k, :], in0=th[0:m, k % 2, :], scalar=0.5, in1=PS[0:m, GB + k % 2, SEQ:2 * SEQ],
                                         op0=ALU.mult, op1=ALU.mult).then_inc(hh_r, 1)

            def final(b, p):
                eng.wait_ge(p_dn, b + 1)
                eng.tensor_tensor(h3[:, p], two(GB), h3[:, p], ALU.add).then_inc(h4_r, 1)

            def step(i, p, pair, front=True, mid=True, back=True, down=True):
                for n in range(SS):
                    if mid:
                        scan(i, n)
                        outputs(i, n)
                    if back and n == 0:
                        residual_f(i - 1, 1 - p)
                    if back and n == 3:
                        low_f(i - 1)
                    if down and n == 4:
                        final(i - 2, p)
                    if back and 5 <= n < 5 + IB:
                        gated(i - 1, n - 5)
                    if front and n == 5:
                        residual_z(i + 1, 1 - p)
                    if front and n == 9:
                        parts(i + 1, 1 - p)
                    if front and n == 10:
                        raw_dt(i + 1, 1 - p)
                    if front and n == 12:
                        make_dt(i + 1, 1 - p)
                    if front and n == 13:
                        make_du(i + 1, 1 - p)

            residual_z(0, 0)
            parts(0, 0)
            raw_dt(0, 0)
            make_dt(0, 0)
            make_du(0, 0)
            run(eng, step)

        @block.tensor
        def _(eng):
            eng.wait_ge(c_in, 8 * 16)
            eng.wait_ge(c_s, 4)
            eng.wait_ge(c_a, 3)

            def scatter(b):
                eng.wait_ge(f_in, (b + 1) * 48)
                if due(b):
                    eng.wait_ge(xb_r, b)
                if due(b - 1):
                    eng.wait_ge(f_r, b - 1)
                for t in range(T):
                    ins = eng.matmul(PS[:, MB + t, :], pt[:, t * P:(t + 1) * P], ol[:, :], start=True, stop=True)
                ins.then_inc(p_sc, 1)

            def features(src, out):
                for t in range(T):
                    for k in range(KB):
                        ins = eng.transpose(PS[:, MB + t, k * P:(k + 1) * P], src[:, t, k * P:(k + 1) * P], ident[:, :])
                ins.then_inc(out, 1)

            def features_z(b):
                eng.wait_ge(zn_r, b + 1)
                eng.wait_ge(h2_r, b + 1)
                features(xn, t_z)

            def projections(b):
                eng.wait_ge(z_r, b + 1)
                for k in range(KB):
                    eng.matmul(PS[0:DTR, MB, 0:SEQ], wp[:, k, 0:DTR], zT[:, k, :], start=(k == 0), stop=(k == KB - 1))
                for k in range(KB):
                    ins = eng.matmul(PS[0:3 * BCR, MB + 1, 0:SEQ], wp[:, k, DTR:DTR + 3 * BCR], zT[:, k, :],
                                     start=(k == 0), stop=(k == KB - 1))
                ins.then_inc(p_pj, 1)

            def dt_product(b):
                eng.wait_ge(dtr_r, b + 1)
                eng.wait_ge(bc_r, b + 1)
                for k in range(KB):
                    ins = eng.matmul(PS[:, MB + k // 2, k % 2 * SEQ:(k % 2 + 1) * SEQ], wdo[:, k * P:(k + 1) * P], dtr[:, :],
                                     start=True, stop=True)
                ins.then_inc(p_dt, 1)

            def broadcasts(b, p, n):
                m = b * SS + n
                eng.wait_ge(bc_r, b + 1)
                if due(m - 1):
                    eng.wait_ge(cx_s, m - 1)
                for j in range(2):
                    ins = eng.matmul(PS[:, CB + n % 2, j * SEQ:(j + 1) * SEQ], sel[:, j * SS + n:j * SS + n + 1].broadcast_to([3 * BCR, P]), bc[:, p, :], start=True, stop=True)
                ins.then_inc(p_bc, 1)

            def output(b, n):
                m = b * SS + n
                if n == 0:
                    if due(b):
                        eng.wait_ge(h3_r, b)
                    eng.wait_ge(z_r, b + 1)
                    for t in range(T):
                        for k in range(KB):
                            ins = eng.matmul(PS[:, YB + t, k * P:(k + 1) * P], zT[:, k, t * P:(t + 1) * P], diag[:, k, :],
                                             start=(k == 0), stop=False, skip_group_check=True)
                    ins.then_inc(p_zd, 1)
                eng.wait_ge(cx_s, m + 1)
                for t in range(T):
                    for k in range(KB):
                        ins = eng.matmul(PS[:, YB + t, k * P:(k + 1) * P], cx[:, n % 2, k, t * P:(t + 1) * P], ident[:, :],
                                         start=False, stop=(n == SS - 1), is_transpose=True, skip_group_check=True)
                ins.then_inc(y_s, 1)

            def features_f(b):
                eng.wait_ge(fn_r, b + 1)
                eng.wait_ge(xb_r, min(b + 2, NB) if isinstance(b, int) else b + 2)
                features(xn, t_f)

            def gate_up(b, k):
                at, m = b * IB + k, rows_of(k)
                eng.wait_ge(f_r, b + 1)
                if k < 2:
                    if due(b):
                        eng.wait_ge(h4_r, b)
                else:
                    if due(at - 1):
                        eng.wait_ge(hh_r, at - 1)
                for j, base in enumerate((WG, WU)):
                    for kb in range(KB):
                        at_w = base + kb * INTER + k * P
                        ins = split_product(eng, PS[0:m, GB + k % 2, j * SEQ:(j + 1) * SEQ],
                                            (wgh[:, at_w:at_w + m], wgl[:, at_w:at_w + m]), (fh[:, kb, :], fl[:, kb, :]),
                                            kb == 0, kb == KB - 1)
                ins.then_inc(p_gu, 1)

            def down_product(b, blocks):
                eng.wait_ge(hh_r, (b + 1) * IB)
                for k in blocks:
                    m = rows_of(k)
                    for t in range(T):
                        ins = eng.matmul(PS[:, GB + t, :], hh[0:m, k, t * P:(t + 1) * P], wd[0:m, k * DM:(k + 1) * DM],
                                         start=(k == 0), stop=(k == IB - 1))
                if blocks[-1] == IB - 1:
                    ins.then_inc(p_dn, 1)

            def step(i, p, pair, front=True, mid=True, back=True, down=True):
                for n in range(SS):
                    if n == 0 and back:
                        output(i - 1, SS - 1)
                    if mid and n > 0:
                        output(i, n - 1)
                    if n in DOWN and (back if n == 15 else down):
                        down_product(i - 1 if n == 15 else i - 2, DOWN[n])
                    if back and 4 <= n < 4 + IB:
                        gate_up(i - 1, n - 4)
                    if back and n == 2:
                        features_f(i - 1)
                    if front and n == 5:
                        scatter(i + 1)
                    if front and n == 7:
                        features_z(i + 1)
                    if front and n == 9:
                        projections(i + 1)
                    if front and n == 10:
                        dt_product(i + 1)
                    if mid and n + 2 < SS:
                        broadcasts(i, p, n + 2)
                    if front and n + 2 >= SS:
                        broadcasts(i + 1, 1 - p, n + 2 - SS)

            scatter(0)
            features_z(0)
            projections(0)
            dt_product(0)
            broadcasts(0, 0, 0)
            broadcasts(0, 0, 1)
            run(eng, step)


def build(nc, d):
    for name, shape, dt in (("hT", [NCH, P, LC * HH * HC], F32), ("hb", [NB, P, T * DM], F32), ("fx", [P, KB, NB * TOPK], F32),
                            ("pt", [TOPK, NB * SEQ], F32), ("ol", [NB * TOPK, DM], F32), ("w", [P, WCOLS], I32)):
        if name not in d:
            d[name] = nc.dram_tensor("scratch_" + name, shape, dt, kind="Internal").ap()
    ctx = ExitStack()
    with ctx:
        PS = ctx.enter_context(nc.psum_tensor("PS", [P, 8, 512], F32))
        ident = ctx.enter_context(nc.sbuf_tensor("ident", [P, P], F32))
        halves = ctx.enter_context(nc.sbuf_tensor("halves", [P, T], F32))
        lut = ctx.enter_context(nc.sbuf_tensor("lut_sb", [P, NLUT], I32))
        made = ctx.enter_context(nc.semaphore("constants_made"))
        loaded = ctx.enter_context(nc.semaphore("table_loaded"))
        apart = [ctx.enter_context(nc.semaphore("apart_" + e)) for e in ("scalar", "vector", "gpsimd")]
        C = {"ident": ident, "halves": halves, "lut": lut, "apart": apart}
        with nc.Block() as block:
            @block.sync
            def _(eng):
                eng.dma_start(lut[:, :].bitcast(F32), d["lut"].unsqueeze(0).broadcast_to([P, NLUT])).then_inc(loaded, 16)
                eng.wait_ge(loaded, 16)

            @block.gpsimd
            def _(eng):
                eng.memset(halves[:, :], -0.5).then_inc(made, 1)
                eng.memset(ident[:, :], 0.0).then_inc(made, 1)
                eng.wait_ge(made, 2)
                eng.affine_select(out=ident[:, :], in_=ident[:, :], compare_op=ALU.not_equal, fill=1.0, base=0,
                                  pattern=[[-1, P]], channel_multiplier=1).then_inc(made, 1)
                eng.wait_ge(made, 3)
        s4d_phase(nc, PS, d)
        attention_phase(nc, PS, d, C)
        C["wgh"] = ctx.enter_context(nc.sbuf_tensor("wgh", [P, WD], F32R))
        C["wgl"] = ctx.enter_context(nc.sbuf_tensor("wgl", [P, WD], F32R))
        C["wd"] = ctx.enter_context(nc.sbuf_tensor("wd", [P, IB * DM], F32))
        routed_ffn_phase(nc, PS, d, C)
        scan_phase(nc, PS, d, C)


def kernel(**inputs):
    import concourse.bacc as bacc
    from concourse.bass_utils import run_bass_kernel_spmd

    x = {k: np.asarray(v) for k, v in inputs.items()}

    def by_state(a):
        return a.reshape(HH, P, NSTATE).transpose(0, 2, 1).reshape(HH * NSTATE, P)

    def by_input(w):
        return w.reshape(KB, P, -1).transpose(1, 0, 2)

    columns = lambda v: v.reshape(KB, P).T
    index = [by_input(x[f"L1_ffn_{n}_idx"].T).reshape(P, -1) for n in ("gate", "up")]
    down = np.zeros((IB * P, DM), np.int32)
    down[:INTER] = x["L1_ffn_down_idx"].T
    index.append(down.reshape(IB, P, DM).transpose(1, 0, 2).reshape(P, -1))
    arrays = {
        "xc": x["x"].reshape(NB, HH, P, NSTATE, 2).transpose(1, 3, 4, 2, 0).reshape(P, 2, P, NB),
        "log_dt": x["L0_tok_log_dt"],
        "inv_A_real": by_state(x["L0_tok_inv_A_real"]), "A_imag": by_state(x["L0_tok_A_imag"]),
        "B_re": by_state(x["L0_tok_B_ri"][..., 0]), "B_im": by_state(x["L0_tok_B_ri"][..., 1]),
        "w_attn": np.stack([by_input(x["L0_attn_" + n].T) for n in ("wq", "wk", "wv", "wo")]),
        "bq": columns(x["L0_attn_bq"]), "bk": x["L0_attn_bk"], "bv": x["L0_attn_bv"], "bo": x["L0_attn_bo"],
        "Wr": x["L0_ffn_Wr"].reshape(DM), "br": x["L0_ffn_br"],
        "W1": x["L0_ffn_W1"].reshape(KB, P, FB, P).transpose(2, 1, 0, 3), "b1": x["L0_ffn_b1"].reshape(FB, P).T,
        "W2": x["L0_ffn_W2"].reshape(FB, P, DM), "b2": x["L0_ffn_b2"],
        "w_dti": by_input(x["L1_attn_W_dt_in"].T),
        "w_bc": by_input(np.concatenate([x["L1_attn_W_B"], x["L1_attn_W_C"]]).T),
        "w_dto": x["L1_attn_W_dt_out"].T, "b_dt": columns(x["L1_attn_b_dt_out"]), "D": columns(x["L1_attn_D"]),
        "A_log": by_input(x["L1_attn_A_log"]),
        "lut": x["L1_ffn_lut"], "idx": np.concatenate(index, 1),
    }
    nc = bacc.Bacc("TRN2", target_bir_lowering=False, num_devices=1)
    feed, d = {}, {}
    for name, a in arrays.items():
        feed["in_" + name] = a = np.ascontiguousarray(a)
        d[name] = nc.dram_tensor("in_" + name, a.shape, mybir.dt.from_np(a.dtype), kind="ExternalInput").ap()
    d["out"] = nc.dram_tensor("out_h", (NB, SEQ, DM), F32, kind="ExternalOutput").ap()
    build(nc, d)
    return run_bass_kernel_spmd(nc, [feed], core_ids=[0]).results[0]["out_h"]
```

```python
import numpy as np
import concourse.bass as bass
from concourse import mybir
from contextlib import ExitStack

F32 = mybir.dt.float32
BF16 = mybir.dt.bfloat16
I32 = mybir.dt.int32
ALU = mybir.AluOpType
ACT = mybir.ActivationFunctionType
AX = mybir.AxisListType

P = 128
NB = 16
SEQ = 256
NSTATE = 64
DM = 512
KB = DM // P
T = SEQ // P
HEADS = 16
DK = DM // HEADS
HPB = P // DK
TOPK = SEQ // 8
DFF = 4 * DM
FB = DFF // P
SS = 16
DTR = 64
INTER = 1376
IB = (INTER + P - 1) // P
ILAST = INTER - (IB - 1) * P
NLUT = 16
EPS = 1e-5

HH = SEQ // P
L0 = P
L1 = DM // L0
HC = 32
NCH = P // HC
LC = L1 * NB
GH = 8
NG = HC // GH
NPOW = 9

WG = 0
WU = KB * INTER
WD = 2 * KB * INTER
WCOLS = WD + IB * DM
WSC = WD // FB
WDC = (WCOLS - WD) // FB
WCH = WD // NB


def due(value):
    return not isinstance(value, int) or value > 0


def each_batch(eng, step, first, last, unroll=2):
    with eng.Fori(first // unroll, last // unroll) as group:
        for q in range(unroll):
            step(group * unroll + q, q, group)


def s4d_phase(nc, PS, d):
    ctx = ExitStack()
    with ctx:
        sb = lambda name, shape, dt=F32: ctx.enter_context(nc.sbuf_tensor("s4_" + name, shape, dt))
        sem = lambda name: ctx.enter_context(nc.semaphore("s4_" + name))
        raw = sb("raw", [P, 5, P])
        xc = sb("xc", [P, 2, 2, HC, NB])
        mid = sb("mid", [P, 10, P])
        PR = sb("PR", [P, NPOW, P])
        PI = sb("PI", [P, NPOW, P])
        NPI = sb("NPI", [P, NPOW, P])
        G = sb("G", [P, 3, P])
        W = sb("W", [P, 2, 2, HC, L0])
        Q = sb("Q", [P, 2, HC, LC])
        QB = sb("QB", [P, 2, HC, HH, LC])
        tmp = sb("tmp", [P, 2, 2, HC, L0 // 2])
        hts = sb("hts", [P, 2, LC, HH, HC])

        loaded = sem("loaded")
        xc_in = [sem(f"xc_in{p}") for p in range(2)]
        e_done = sem("e_done")
        par = sem("par")
        ones_set = sem("ones_set")
        cm = sem("cm")
        qb_zero = sem("qb_zero")
        qb_ready = sem("qb_ready")
        prod = sem("prod")
        evac = sem("evac")
        stored = [sem(f"stored{p}") for p in range(2)]
        c_used = sem("c_used")

        steps = 2 + 6 * 4 + 4 + 2 * 4
        dt, ea, a, b, om, op, D, rD, t0, t1 = (mid[:, j, :] for j in range(10))
        s = ea
        block = ctx.enter_context(nc.Block())

        @block.sync
        def _(eng):
            for hh in range(HH):
                eng.dma_start(raw[hh * NSTATE:(hh + 1) * NSTATE, 0, :],
                              d["log_dt"][hh * P:(hh + 1) * P].unsqueeze(0).broadcast_to([NSTATE, P])).then_inc(loaded, 16)
            for j, name in enumerate(["inv_A_real", "A_imag", "B_re", "B_im"]):
                eng.dma_start(raw[:, 1 + j, :], d[name]).then_inc(loaded, 16)

            def chunk(i, p, half):
                if due(i - 1):
                    eng.wait_ge(c_used, i - 1)
                for ri in range(2):
                    eng.dma_start(xc[:, p, ri, :, :], d["xc"][:, ri, bass.ds(i * HC, HC), :]).then_inc(xc_in[p], 16)
            chunk(0, 0, 0)
            chunk(1, 1, 0)
            each_batch(eng, chunk, 2, NCH)

        @block.scalar
        def _(eng):
            eng.wait_ge(loaded, 6 * 16)
            eng.activation(dt, raw[:, 0, :], ACT.Exp).then_inc(e_done, 1)
            eng.activation(ea, raw[:, 1, :], ACT.Exp).then_inc(e_done, 1)
            eng.wait_ge(qb_zero, 1)

            def chunk(i, p, half):
                if due(i * NG):
                    eng.wait_ge(prod, i * NG)
                eng.wait_ge(cm, (i + 1) * steps)
                for g in range(NG):
                    cols = slice(g * GH, (g + 1) * GH)
                    for hh in range(HH):
                        rows = slice(hh * NSTATE, (hh + 1) * NSTATE)
                        eng.activation(QB[rows, :, cols, hh, :], Q[rows, :, cols], ACT.Copy).then_inc(qb_ready, 1)
                if due(half * 16):
                    eng.wait_ge(stored[p], half * 16)
                for g in range(NG):
                    eng.wait_ge(prod, i * NG + g + 1)
                    for r in range(2):
                        last = eng.activation(
                            hts[:, p, :, :, g * GH + r * GH // 2:g * GH + (r + 1) * GH // 2],
                            PS[:, 2 * g + r, :].rearrange("p (h x q) -> p q x h", x=HH, q=LC), ACT.Copy)
                    last.then_inc(evac, 1)
            chunk(0, 0, 0)
            chunk(1, 1, 0)
            each_batch(eng, chunk, 2, NCH)

        @block.gpsimd
        def _(eng):
            eng.memset(QB[:, :, :, :, :], 0.0).then_inc(qb_zero, 1)

            def chunk(i, p, half):
                eng.wait_ge(evac, (i + 1) * NG)
                eng.dma_start(d["hT"][bass.ds(i, 1)], hts[:, p].rearrange("p q a b -> p (q a b)")).then_inc(stored[p], 16)
            for p in range(2):
                chunk(p, p, 0)
            each_batch(eng, chunk, 2, NCH)
            for p in range(2):
                eng.wait_ge(stored[p], NCH // 2 * 16)

        @block.vector
        def _(eng):
            n = 0

            def done(ins):
                nonlocal n
                n += 1
                ins.then_inc(par, 1)
                eng.wait_ge(par, n)

            for p in range(2):
                eng.memset(W[:, p, 0, :, 0:1], 1.0).then_inc(ones_set, 1)
                eng.memset(W[:, p, 1, :, 0:1], 0.0).then_inc(ones_set, 1)
            eng.wait_ge(loaded, 6 * 16)
            eng.wait_ge(e_done, 2)
            done(eng.scalar_tensor_tensor(out=a, in0=ea, scalar=-0.5, in1=dt, op0=ALU.mult, op1=ALU.mult))
            done(eng.scalar_tensor_tensor(out=b, in0=raw[:, 2, :], scalar=0.5, in1=dt, op0=ALU.mult, op1=ALU.mult))
            done(eng.tensor_scalar(om, a, -1.0, 1.0, ALU.mult, ALU.add))
            done(eng.tensor_scalar(op, a, 1.0, None, ALU.add))
            done(eng.tensor_tensor(t0, om, om, ALU.mult))
            done(eng.tensor_tensor(t1, b, b, ALU.mult))
            done(eng.tensor_tensor(D, t0, t1, ALU.add))
            done(eng.reciprocal(rD, D))
            done(eng.tensor_tensor(t0, om, op, ALU.mult))
            done(eng.tensor_tensor(t0, t0, t1, ALU.subtract))
            done(eng.tensor_tensor(PR[:, 0, :], t0, rD, ALU.mult))
            done(eng.scalar_tensor_tensor(out=PI[:, 0, :], in0=b, scalar=2.0, in1=rD, op0=ALU.mult, op1=ALU.mult))
            done(eng.scalar_tensor_tensor(out=s, in0=dt, scalar=2.0, in1=rD, op0=ALU.mult, op1=ALU.mult))
            Br, Bi = raw[:, 3, :], raw[:, 4, :]
            done(eng.tensor_tensor(t0, Br, om, ALU.mult))
            done(eng.tensor_tensor(t1, Bi, b, ALU.mult))
            done(eng.tensor_tensor(t0, t0, t1, ALU.subtract))
            done(eng.tensor_tensor(G[:, 0, :], t0, s, ALU.mult))
            done(eng.tensor_tensor(t0, Br, b, ALU.mult))
            done(eng.tensor_tensor(t1, Bi, om, ALU.mult))
            done(eng.tensor_tensor(t0, t0, t1, ALU.add))
            done(eng.scalar_tensor_tensor(out=G[:, 1, :], in0=t0, scalar=-1.0, in1=s, op0=ALU.mult, op1=ALU.mult))
            done(eng.tensor_scalar(G[:, 2, :], G[:, 0, :], -1.0, None, ALU.mult))
            for k in range(1, NPOW):
                pr, pi = PR[:, k - 1, :], PI[:, k - 1, :]
                done(eng.tensor_tensor(t0, pr, pi, ALU.subtract))
                done(eng.tensor_tensor(t1, pr, pi, ALU.add))
                done(eng.tensor_tensor(PR[:, k, :], t0, t1, ALU.mult))
                done(eng.scalar_tensor_tensor(out=PI[:, k, :], in0=pr, scalar=2.0, in1=pi, op0=ALU.mult, op1=ALU.mult))
            done(eng.tensor_scalar(NPI[:, :, :], PI[:, :, :], -1.0, None, ALU.mult))
            eng.wait_ge(ones_set, 4)

            def power(table, k, i, cols):
                return table[:, k, bass.ds(i * HC, HC)].unsqueeze(2).broadcast_to([P, HC, cols])

            def both(ap, cols):
                return ap.unsqueeze(1).broadcast_to([P, 2, HC, cols])

            def chunk(i, p, half):
                at = 0

                def step(ins):
                    nonlocal at
                    at += 1
                    ins.then_inc(cm, 1)

                def settle():
                    eng.wait_ge(cm, i * steps + at)

                def times(out, src, k, cols, conj):
                    pr = power(PR, k, i, cols)
                    plus, minus = (power(NPI, k, i, cols), power(PI, k, i, cols)) if conj else (power(PI, k, i, cols), power(NPI, k, i, cols))
                    t, v = tmp[:, 0, :, :, 0:cols], tmp[:, 1, :, :, 0:cols]
                    step(eng.tensor_tensor(t, src, both(pr, cols), ALU.mult))
                    step(eng.tensor_tensor(v[:, 0], src[:, 1], minus, ALU.mult))
                    step(eng.tensor_tensor(v[:, 1], src[:, 0], plus, ALU.mult))
                    settle()
                    step(eng.tensor_tensor(out, t, v, ALU.add))
                    settle()

                if due((i - 1) * NG):
                    eng.wait_ge(prod, (i - 1) * NG)
                w, q = W[:, p], Q
                step(eng.tensor_copy(w[:, 0, :, 1:2], PR[:, 0, bass.ds(i * HC, HC)].unsqueeze(2)))
                step(eng.tensor_copy(w[:, 1, :, 1:2], PI[:, 0, bass.ds(i * HC, HC)].unsqueeze(2)))
                settle()
                for k in range(1, 7):
                    m = 2 ** k
                    times(w[:, :, :, m:2 * m], w[:, :, :, 0:m], k, m, False)
                eng.wait_ge(xc_in[p], (half + 1) * 32)
                c = xc[:, p]
                g = lambda j: G[:, j, bass.ds(i * HC, HC)].unsqueeze(2).broadcast_to([P, HC, NB])
                t, v = tmp[:, 0, :, :, 0:NB], tmp[:, 1, :, :, 0:NB]
                if due(i * NG * HH):
                    eng.wait_ge(qb_ready, i * NG * HH)
                step(eng.tensor_tensor(t[:, 0], c[:, 0], g(0), ALU.mult))
                step(eng.tensor_tensor(t[:, 1], c[:, 0], g(1), ALU.mult))
                step(eng.tensor_tensor(v[:, 0], c[:, 1], g(1), ALU.mult))
                step(eng.tensor_tensor(v[:, 1], c[:, 1], g(2), ALU.mult))
                settle()
                eng.tensor_tensor(q[:, :, :, 0:NB], t, v, ALU.add).then_inc(c_used, 1)
                eng.wait_ge(c_used, i + 1)
                times(q[:, :, :, NB:2 * NB], q[:, :, :, 0:NB], 7, NB, True)
                times(q[:, :, :, 2 * NB:4 * NB], q[:, :, :, 0:2 * NB], 8, 2 * NB, True)
                assert at == steps

            for p in range(2):
                chunk(p, p, 0)
            each_batch(eng, chunk, 2, NCH)

        @block.tensor
        def _(eng):
            def chunk(i, p, half):
                for g in range(NG):
                    eng.wait_ge(qb_ready, (i * NG + g + 1) * HH)
                    if due((i - 1) * NG + g + 1):
                        eng.wait_ge(evac, (i - 1) * NG + g + 1)
                    for r in range(GH):
                        bank, at = 2 * g + r // (GH // 2), r % (GH // 2) * HH * LC
                        for ri in range(2):
                            mm = eng.matmul(PS[:, bank, at:at + HH * LC], W[:, p, ri, g * GH + r, :],
                                            QB[:, ri, g * GH + r, :, :], start=(ri == 0), stop=(ri == 1))
                    mm.then_inc(prod, 1)
            for p in range(2):
                chunk(p, p, 0)
            each_batch(eng, chunk, 2, NCH)
F32R = mybir.dt.float32r
VA = P + HPB
HSLOTS = 4
LW = WCH // 2


def split_product(eng, out, left, right, start, stop, **kw):
    (lh, ll), (rh, rl) = left, right
    eng.matmul(out, ll, rh, start=start, stop=False, **kw)
    eng.matmul(out, lh, rl, start=False, stop=False, **kw)
    return eng.matmul(out, lh, rh, start=False, stop=stop, **kw)


def inverse_root(eng, wait_value, stats, mv, ve, rs, nm, halves, free, steps, n, out, apart):
    eng.wait_ge(stats, wait_value)
    if due(n):
        eng.wait_ge(free, n)
        eng.sem_inc(apart, 1)
    eng.tensor_scalar(ve, mv[:, :, 1], EPS, None, ALU.add).then_inc(steps, 1)
    eng.wait_ge(steps, n * 3 + 1)
    eng.tensor_tensor(rs, ve, halves[:, 0:T], ALU.pow).then_inc(steps, 1)
    eng.wait_ge(steps, n * 3 + 2)
    eng.tensor_tensor(ve, mv[:, :, 0], rs, ALU.mult).then_inc(steps, 1)
    eng.wait_ge(steps, n * 3 + 3)
    eng.sem_inc(apart, 1)
    eng.tensor_scalar(nm, ve, -1.0, None, ALU.mult).then_inc(out, 1)


def statistics(eng, tiles, st, mv, steps, n, out, apart):
    for t in range(T):
        eng.bn_stats(st[:, t, :], tiles[t]).then_inc(steps, 1)
    eng.wait_ge(steps, (n + 1) * T)
    eng.sem_inc(apart, 1)
    for t in range(T):
        ins = eng.bn_aggr(mv[:, t, :], st[:, t, :])
    ins.then_inc(out, 1)


L_STEPS = 13


def table_bits(eng, x, lm, lx, pairs, lut, steps, used, n):
    eng.tensor_scalar(lm[:, 0], x, 31, 31, ALU.logical_shift_left, ALU.arith_shift_right).then_inc(steps, 1)
    for b in range(1, 4):
        eng.tensor_scalar(lm[:, b], x, 1 << b, None, ALU.bitwise_and).then_inc(used if b == 3 else steps, 1)
    eng.wait_ge(steps, n * L_STEPS + 1)
    for j in range(NLUT // 2):
        eng.tensor_scalar(lx[:, j, :], lm[:, 0], pairs[:, j:j + 1], lut[:, 2 * j:2 * j + 1],
                          ALU.bitwise_and, ALU.bitwise_xor).then_inc(steps, 1)


def table_choice(eng, lm, lx, width, steps, used, n, out, apart, levels=(1, 2, 3)):
    for b in levels:
        eng.wait_ge(steps, n * L_STEPS + 10 + b)
        if b == 1:
            eng.wait_ge(used, n + 1)
        eng.sem_inc(apart, 1)
        left = NLUT >> (b + 1)
        two = lx.rearrange("p (n two s) c -> p n two s c", two=2, s=1 << (b - 1))
        eng.copy_predicated(two[:, :, 0, 0, :], lm[:, b].unsqueeze(1).broadcast_to([P, left, width]),
                            two[:, :, 1, 0, :]).then_inc(steps if b < 3 else out, 1)


def attention_phase(nc, PS, d, C):
    ctx = ExitStack()
    with ctx:
        sb = lambda name, shape, dt=F32: ctx.enter_context(nc.sbuf_tensor("at_" + name, shape, dt))
        sem = lambda name: ctx.enter_context(nc.semaphore("at_" + name))
        ident, halves = C["ident"], C["halves"]
        WH = sb("WH", [P, 4, KB, DM], F32R)
        WL = sb("WL", [P, 4, KB, DM], F32R)
        bq = sb("bq", [P, KB])
        bk = sb("bk", [P, DM])
        bv = sb("bv", [P, DM])
        bo = sb("bo", [P, DM])
        wr = sb("wr", [P, DM])
        br = sb("br", [P, 1])
        mask = sb("mask", [P, VA])
        before = sb("before", [P, T, SEQ])
        ones = sb("ones", [P, SEQ])
        slot = sb("slot", [P, TOPK])
        hT = sb("hT", [P, HSLOTS, KB, SEQ])
        st1 = sb("st1", [P, T, 6])
        mv1 = sb("mv1", [P, T, 2])
        ve1 = sb("ve1", [P, T])
        rs1 = sb("rs1", [P, T])
        nm1 = sb("nm1", [P, T])
        st2 = sb("st2", [P, T, 6])
        mv2 = sb("mv2", [P, T, 2])
        ve2 = sb("ve2", [P, T])
        rs2 = sb("rs2", [P, T])
        nm2 = sb("nm2", [P, T])
        xn = sb("xn", [P, T, DM])
        xh = sb("xh", [P, KB, SEQ], F32R)
        xl = sb("xl", [P, KB, SEQ], F32R)
        qe = sb("qe", [P, KB, SEQ])
        qr = sb("qr", [P, KB, SEQ])
        q = sb("q", [P, KB, SEQ])
        kx = sb("kx", [P, T, DM])
        ke = sb("ke", [P, T, DM])
        kf = sb("kf", [P, T, DM])
        va = sb("va", [P, T, KB, VA])
        kv = sb("kv", [P, KB, VA])
        den = sb("den", [P, T, HEADS])
        at = sb("at", [P, T, DM])
        ah = sb("ah", [P, KB, SEQ], F32R)
        al = sb("al", [P, KB, SEQ], F32R)
        h1 = sb("h1", [P, 2, T, DM])
        yn = sb("yn", [P, T, DM])
        hb = sb("hb", [P, T, DM])
        junk = sb("junk", [P, DM])
        lg0 = sb("lg0", [P, T])
        lg = sb("lg", [P, T])
        cnt = sb("cnt", [P, 2, T])
        rank = sb("rank", [P, T])
        mx = sb("mx", [P, 1])
        nmx = sb("nmx", [P, 1])
        ex = sb("ex", [P, T])
        es = sb("es", [P, T])
        rz = sb("rz", [P, 1])
        rw = sb("rw", [P, T])
        oh = sb("oh", [P, T, TOPK])
        ow = sb("ow", [P, T, TOPK])
        fx = sb("fx", [P, KB, TOPK])
        pt = sb("pt", [TOPK, SEQ])
        li = sb("li", [P, 2, LW], I32)
        lm = sb("lm", [P, 4, LW], I32)
        lx = sb("lx", [P, 2, NLUT // 2, LW], I32)
        stage = lx[:, :, :, :].bitcast(F32).rearrange("p a b c -> p (a b c)")[:, 0:2 * KB * DM].rearrange(
            "p (a k n) -> p a k n", a=2, k=KB)

        w_in = [sem(f"w_in{p}") for p in range(2)]
        c_in = sem("c_in")
        w_high = sem("w_high")
        w_low = sem("w_low")
        const_s = sem("const_s")
        h_in = [sem(f"h_in{q}") for q in range(HSLOTS)]
        st1_s, mv1_r, root1_s, rs1_r = sem("st1_s"), sem("mv1_r"), sem("root1_s"), sem("rs1_r")
        st2_s, mv2_r, root2_s, rs2_r = sem("st2_s"), sem("mv2_r"), sem("root2_s"), sem("rs2_r")
        t_h, xn_r, t_x, x_high, x_low = sem("t_h"), sem("xn_r"), sem("t_x"), sem("x_high"), sem("x_low")
        p_q, p_k, p_v = sem("p_q"), sem("p_k"), sem("p_v")
        q_exp, q_r, k_sum, k_exp, k_s, k_r, v_r = (sem(n) for n in ("q_exp", "q_r", "k_sum", "k_exp", "k_s", "k_r", "v_r"))
        p_kv, kv_r, p_a, a_s, a_r, t_a, a_high, a_low = (
            sem(n) for n in ("p_kv", "kv_r", "p_a", "a_s", "a_r", "t_a", "a_high", "a_low"))
        p_o, h1_r, y_r, hb_r = sem("p_o"), sem("h1_r"), sem("y_r"), sem("hb_r")
        lg_s, lg_r, p_row, r_s, mx_r, oh_r = (sem(n) for n in ("lg_s", "lg_r", "p_row", "r_s", "mx_r", "oh_r"))
        ex_r, es_r, p_g, w_s, ow_r, fx_r, p_t, pt_r = (
            sem(n) for n in ("ex_r", "es_r", "p_g", "w_s", "ow_r", "fx_r", "p_t", "pt_r"))
        s_hb, s_fx, s_pt = sem("s_hb"), sem("s_fx"), sem("s_pt")
        l_in = [sem(f"l_in{p}") for p in range(2)]
        l_out = [sem(f"l_out{p}") for p in range(2)]
        l_used, l_s, l_r = sem("l_used"), sem("l_s"), sem("l_r")

        _, v_apart, g_apart = C["apart"]

        WQ, WK, WV, WO = range(4)
        two = lambda b: PS[:, b:b + 2, :]
        SUMS = (0, 6)

        def sums_of(t):
            return PS[:, SUMS[t]:SUMS[t] + 2, 0:2 * VA].rearrange("p b (c v) -> p b c v", c=2)

        def run(eng, step):
            def at(i, q, group, **kw):
                step(i, q % 2, (q, group), **kw)
            for q in range(HSLOTS):
                at(q, q, 0, tail=(q > 0))
            each_batch(eng, at, HSLOTS, NB - HSLOTS, HSLOTS)
            for q in range(HSLOTS):
                at(NB - HSLOTS + q, q, NB // HSLOTS - 1, head=(q < HSLOTS - 1))

        block = ctx.enter_context(nc.Block())

        @block.sync
        def _(eng):
            hsrc = d["hT"].rearrange("j p (k c x a) -> p k c x j a", k=L1, c=NB, x=HH)

            def load_h(i, q):
                if due(i - HSLOTS + 1):
                    eng.wait_ge(p_o, i - HSLOTS + 1)
                for hh in range(HH):
                    for k in range(KB):
                        eng.dma_start(hT[:, q, k, hh * P:(hh + 1) * P].rearrange("p (j a) -> p j a", j=NCH),
                                      hsrc[:, k, i, hh]).then_inc(h_in[q], 16)

            def load_index(i, half):
                if due(i * 2 + half - 1):
                    eng.wait_ge(l_used, i * 2 + half - 1)
                eng.dma_start(li[:, half, :], d["idx"][:, bass.ds(i * WCH + half * LW, LW)]).then_inc(l_in[half], 16)

            def store_weights(i, half):
                eng.wait_ge(l_r, i * 2 + half + 1)
                eng.dma_start(d["w"][:, bass.ds(i * WCH + half * LW, LW)], lx[:, half, 0, :]).then_inc(l_out[half], 16)

            for j in range(4):
                if due(j - 1):
                    eng.wait_ge(w_low, j - 1)
                eng.dma_start(stage[:, j % 2], d["w_attn"][j]).then_inc(w_in[j % 2], 16)
                if j == 0:
                    load_h(0, 0)
                    load_h(1, 1)
                if j == 1:
                    eng.dma_start(bq[:, :], d["bq"]).then_inc(c_in, 16)
                    for tile, name in ((bk, "bk"), (bv, "bv"), (bo, "bo"), (wr, "Wr"), (br, "br")):
                        eng.dma_start(tile[:, :], d[name].unsqueeze(0).broadcast_to([P, tile.shape[1]])).then_inc(c_in, 16)
                    load_index(0, 0)
                    load_index(0, 1)

            def step(i, p, place, head=True, tail=True):
                hq = place[0]
                if not isinstance(i, int) or i + 2 < NB:
                    load_h(i + 2, (hq + 2) % HSLOTS)
                for half in range(2):
                    if head:
                        load_index(i + 1, half)
                    store_weights(i, half)
            run(eng, step)
            for half in range(2):
                eng.wait_ge(l_out[half], NB * 16)

        @block.gpsimd
        def _(eng):
            eng.memset(mask[:, :], 0.0).then_inc(const_s, 1)
            eng.memset(before[:, :, :], 1.0).then_inc(const_s, 1)
            eng.memset(ones[:, :], 1.0).then_inc(const_s, 1)
            eng.iota(slot[:, :], [[1, TOPK]], base=0, channel_multiplier=0,
                     allow_small_or_imprecise_dtypes=True).then_inc(const_s, 1)
            for t in range(T):
                eng.memset(va[:, t, :, P:VA], 1.0).then_inc(const_s, 1)
            eng.wait_ge(const_s, 6)
            for h in range(HPB):
                rows = slice(h * DK, (h + 1) * DK)
                eng.memset(mask[rows, rows], 1.0).then_inc(const_s, 1)
                eng.memset(mask[rows, P + h:P + h + 1], 1.0).then_inc(const_s, 1)
                eng.wait_ge(const_s, 8 + 2 * h)
            eng.affine_select(out=before[:, :, :], in_=before[:, :, :], compare_op=ALU.is_gt, fill=0.0,
                              base=0, pattern=[[P, T], [-1, SEQ]], channel_multiplier=1).then_inc(const_s, 1)

            def root_h(i):
                inverse_root(eng, i + 1, mv1_r, mv1, ve1[:, :], rs1[:, :], nm1[:, :], halves, xn_r, root1_s, i, rs1_r, g_apart)

            def router(i, p):
                inverse_root(eng, i + 1, mv2_r, mv2, ve2[:, :], rs2[:, :], nm2[:, :], halves, y_r, root2_s, i, rs2_r, g_apart)
                eng.wait_ge(y_r, i + 1)
                if due(i * 16):
                    eng.wait_ge(s_hb, i * 16)
                eng.tensor_tensor(hb[:, :, :], h1[:, p], yn[:, :, :], ALU.add).then_inc(hb_r, 1)
                eng.wait_ge(hb_r, i + 1)
                eng.dma_start(d["hb"][i], hb[:, :, :].rearrange("p t d -> p (t d)")).then_inc(s_hb, 16)

            def step(i, p, place, head=True, tail=True):
                if tail:
                    router(i - 1, 1 - p)
                if head:
                    root_h(i + 1)
            root_h(0)
            run(eng, step)
            router(NB - 1, 1)
            eng.wait_ge(s_hb, NB * 16)

        @block.scalar
        def _(eng):
            def high_of_weight(j):
                eng.wait_ge(w_in[j % 2], (j // 2 + 1) * 16)
                eng.activation(WH[:, j], stage[:, j % 2], ACT.Copy).then_inc(w_high, 1)

            def normalise(i):
                eng.wait_ge(rs1_r, i + 1)
                if due(i):
                    eng.wait_ge(t_x, i)
                for t in range(T):
                    ins = eng.activation(xn[:, t, :], PS[:, 6 + t, :], ACT.Identity, bias=nm1[:, t:t + 1],
                                         scale=rs1[:, t:t + 1])
                ins.then_inc(xn_r, 1)

            def high_of_x(i):
                eng.wait_ge(t_x, i + 1)
                if due(i):
                    eng.wait_ge(p_v, i)
                eng.activation(xh[:, :, :].rearrange("p k s -> p (k s)"), two(4).rearrange("p b s -> p (b s)"), ACT.Copy).then_inc(x_high, 1)

            def router_input(i, p):
                eng.wait_ge(rs2_r, i + 1)
                if due(i):
                    eng.wait_ge(p_g, i)
                if due(i):
                    eng.wait_ge(hb_r, i)
                if due(i):
                    eng.wait_ge(lg_r, i)
                for t in range(T):
                    ins = eng.activation(yn[:, t, :], h1[:, p, t, :], ACT.Identity, bias=nm2[:, t:t + 1],
                                         scale=rs2[:, t:t + 1])
                ins.then_inc(y_r, 1)

            def exponents(i):
                eng.wait_ge(mx_r, i + 1)
                if due(i):
                    eng.wait_ge(es_r, i)
                eng.activation(ex[:, :], lg[:, :], ACT.Exp, bias=nmx[:, 0:1]).then_inc(ex_r, 1)

            def gathered(i):
                eng.wait_ge(p_g, i + 1)
                if due(i * 16):
                    eng.wait_ge(s_fx, i * 16)
                eng.activation(fx[:, :, :].rearrange("p k r -> p (k r)"), PS[:, 3, 0:KB * TOPK], ACT.Copy).then_inc(fx_r, 1)
                eng.wait_ge(fx_r, i + 1)
                eng.dma_start(d["fx"][:, :, bass.ds(i * TOPK, TOPK)], fx[:, :, :]).then_inc(s_fx, 16)

            def spreading(i):
                eng.wait_ge(p_t, i + 1)
                if due(i * 16):
                    eng.wait_ge(s_pt, i * 16)
                eng.activation(pt[:, :], PS[0:TOPK, 2, 0:SEQ], ACT.Copy).then_inc(pt_r, 1)
                eng.wait_ge(pt_r, i + 1)
                eng.dma_start(d["pt"][:, bass.ds(i * SEQ, SEQ)], pt[:, :]).then_inc(s_pt, 16)

            def step(i, p, place, head=True, tail=True):
                eng.wait_ge(p_q, i + 1)
                if due(i):
                    eng.wait_ge(q_r, i)
                for ob in range(KB):
                    src = PS[:, ob // 2, ob % 2 * SEQ:(ob % 2 + 1) * SEQ]
                    eng.activation(qe[:, ob], src, ACT.Exp, bias=bq[:, ob:ob + 1])
                    ins = eng.activation(qr[:, ob], src, ACT.Relu, bias=bq[:, ob:ob + 1])
                ins.then_inc(q_exp, 1)
                if tail:
                    router_input(i - 1, 1 - p)
                eng.wait_ge(k_sum, i + 1)
                if due(i):
                    eng.wait_ge(k_r, i)
                eng.activation(ke[:, :, :], kx[:, :, :], ACT.Exp).then_inc(k_exp, 1)
                if head:
                    normalise(i + 1)
                if tail:
                    exponents(i - 1)
                if head:
                    high_of_x(i + 1)
                if tail:
                    gathered(i - 1)
                eng.wait_ge(t_a, i + 1)
                if due(i):
                    eng.wait_ge(p_o, i)
                eng.activation(ah[:, :, :].rearrange("p k s -> p (k s)"), two(4).rearrange("p b s -> p (b s)"), ACT.Copy).then_inc(a_high, 1)
                if tail:
                    spreading(i - 1)

            high_of_weight(0)
            high_of_weight(1)
            normalise(0)
            high_of_x(0)
            high_of_weight(2)
            high_of_weight(3)
            eng.wait_ge(c_in, 6 * 16)
            run(eng, step)
            router_input(NB - 1, 1)
            exponents(NB - 1)
            gathered(NB - 1)
            spreading(NB - 1)
            eng.wait_ge(s_fx, NB * 16)
            eng.wait_ge(s_pt, NB * 16)

        @block.vector
        def _(eng):
            def low_of_weight(j):
                eng.wait_ge(w_high, j + 1)
                eng.tensor_tensor(WL[:, j], stage[:, j % 2], WH[:, j].bitcast(F32), ALU.subtract).then_inc(w_low, 1)

            def bits(i, half):
                eng.wait_ge(l_in[half], (i + 1) * 16)
                if due(i * 16):
                    eng.wait_ge(l_out[half], i * 16)
                if due(i * 2 + half):
                    eng.wait_ge(l_r, i * 2 + half)
                table_bits(eng, li[:, half, :], lm, lx[:, half], C["pairs"], C["lut"], l_s, l_used, i * 2 + half)

            def choose(i, half, levels=(1, 2, 3)):
                table_choice(eng, lm, lx[:, half], LW, l_s, l_used, i * 2 + half, l_r, v_apart, levels)

            def stats_h(i):
                eng.wait_ge(t_h, i + 1)
                if due(i):
                    eng.wait_ge(rs1_r, i)
                statistics(eng, [PS[:, 6 + t, :] for t in range(T)], st1, mv1, st1_s, i, mv1_r, v_apart)

            def low_of_x(i):
                eng.wait_ge(x_high, i + 1)
                if due(i):
                    eng.wait_ge(p_v, i)
                eng.tensor_tensor(xl[:, :, :].rearrange("p k s -> p (k s)"), two(4).rearrange("p b s -> p (b s)"),
                                  xh[:, :, :].bitcast(F32).rearrange("p k s -> p (k s)"), ALU.subtract).then_inc(x_low, 1)

            def stats_h1(i, p):
                eng.wait_ge(h1_r, i + 1)
                if due(i):
                    eng.wait_ge(rs2_r, i)
                statistics(eng, [h1[:, p, t, :] for t in range(T)], st2, mv2, st2_s, i, mv2_r, v_apart)

            def logits(i):
                eng.wait_ge(y_r, i + 1)
                if due(i):
                    eng.wait_ge(p_row, i)
                if due(i):
                    eng.wait_ge(ex_r, i)
                for t in range(T):
                    eng.scalar_tensor_tensor(out=junk[:, :], in0=yn[:, t, :], scalar=1.0, in1=wr[:, :], op0=ALU.mult,
                                             op1=ALU.mult, accum_out=lg0[:, t:t + 1]).then_inc(lg_s, 1)
                    eng.wait_ge(lg_s, i * T + t + 1)
                eng.tensor_scalar(lg[:, :], lg0[:, :], br[:, 0:1], None, ALU.add).then_inc(lg_r, 1)

            def ranks(i):
                eng.wait_ge(p_row, i + 1)
                eng.wait_ge(lg_r, i + 1)
                if due(i):
                    eng.wait_ge(ow_r, i)
                row = PS[:, 2, 0:SEQ]
                base = i * 6
                for t in range(T):
                    eng.scalar_tensor_tensor(out=junk[:, 0:SEQ], in0=row, scalar=lg[:, t:t + 1], in1=ones[:, :],
                                             op0=ALU.is_gt, op1=ALU.mult, accum_out=cnt[:, 0, t:t + 1]).then_inc(r_s, 1)
                    eng.wait_ge(r_s, base + 2 * t + 1)
                    eng.scalar_tensor_tensor(out=junk[:, 0:SEQ], in0=row, scalar=lg[:, t:t + 1], in1=before[:, t, :],
                                             op0=ALU.is_equal, op1=ALU.mult, accum_out=cnt[:, 1, t:t + 1]).then_inc(r_s, 1)
                    eng.wait_ge(r_s, base + 2 * t + 2)
                eng.tensor_reduce(mx[:, :], row, AX.X, ALU.max).then_inc(r_s, 1)
                eng.tensor_tensor(rank[:, :], cnt[:, 0, :], cnt[:, 1, :], ALU.add).then_inc(r_s, 1)
                eng.wait_ge(r_s, base + 6)
                eng.tensor_scalar(nmx[:, :], mx[:, :], -1.0, None, ALU.mult).then_inc(mx_r, 1)
                if due(i):
                    eng.wait_ge(p_g, i)
                for t in range(T):
                    ins = eng.tensor_scalar(oh[:, t, :], slot[:, :], rank[:, t:t + 1], None, ALU.is_equal)
                ins.then_inc(oh_r, 1)

            def taken(i):
                eng.wait_ge(ex_r, i + 1)
                eng.scalar_tensor_tensor(out=es[:, :], in0=rank[:, :], scalar=float(TOPK), in1=ex[:, :],
                                         op0=ALU.is_lt, op1=ALU.mult).then_inc(es_r, 1)

            def weights(i):
                eng.wait_ge(p_g, i + 1)
                base = i * 2
                eng.reciprocal(rz[:, :], PS[:, 2, SEQ:SEQ + 1]).then_inc(w_s, 1)
                eng.wait_ge(w_s, base + 1)
                eng.tensor_scalar(rw[:, :], es[:, :], rz[:, 0:1], None, ALU.mult).then_inc(w_s, 1)
                eng.wait_ge(w_s, base + 2)
                eng.wait_ge(oh_r, i + 1)
                if due(i):
                    eng.wait_ge(p_t, i)
                for t in range(T):
                    ins = eng.tensor_scalar(ow[:, t, :], oh[:, t, :], rw[:, t:t + 1], None, ALU.mult)
                ins.then_inc(ow_r, 1)

            def step(i, p, place, head=True, tail=True):
                if tail:
                    stats_h1(i - 1, 1 - p)
                eng.wait_ge(q_exp, i + 1)
                if due(i):
                    eng.wait_ge(p_a, i)
                eng.scalar_tensor_tensor(out=q[:, :, :], in0=qe[:, :, :], scalar=1.0, in1=qr[:, :, :], op0=ALU.min,
                                         op1=ALU.add).then_inc(q_r, 1)
                eng.wait_ge(p_k, i + 1)
                eng.tensor_tensor(kx[:, :, :], two(2), bk[:, :].unsqueeze(1).broadcast_to([P, T, DM]), ALU.add).then_inc(k_sum, 1)
                if head:
                    stats_h(i + 1)
                eng.wait_ge(k_exp, i + 1)
                eng.tensor_scalar(kx[:, :, :], kx[:, :, :], 0.0, None, ALU.max).then_inc(k_s, 1)
                eng.wait_ge(k_s, i + 1)
                if tail:
                    logits(i - 1)
                if due(i):
                    eng.wait_ge(p_kv, i)
                eng.scalar_tensor_tensor(out=kf[:, :, :], in0=ke[:, :, :], scalar=1.0, in1=kx[:, :, :], op0=ALU.min,
                                         op1=ALU.add).then_inc(k_r, 1)
                eng.wait_ge(p_v, i + 1)
                for t in range(T):
                    ins = eng.tensor_tensor(va[:, t, :, 0:P], PS[:, 4 + t, :].rearrange("p (b v) -> p b v", b=KB),
                                            bv[:, :].rearrange("p (b v) -> p b v", b=KB), ALU.add)
                ins.then_inc(v_r, 1)
                if tail:
                    ranks(i - 1)
                eng.wait_ge(p_kv, i + 1)
                if due(i):
                    eng.wait_ge(p_a, i)
                eng.tensor_tensor(kv[:, :, :].rearrange("p (b c) v -> p b c v", c=2), sums_of(0),
                                  mask[:, :].unsqueeze(1).unsqueeze(1).broadcast_to([P, 2, 2, VA]), ALU.mult).then_inc(kv_r, 1)
                if tail:
                    taken(i - 1)
                if head:
                    low_of_x(i + 1)
                choose(i, 0, (1,))
                eng.wait_ge(p_a, i + 1)
                for t in range(T):
                    eng.tensor_scalar(den[:, t, :].rearrange("p (b c h) -> p b c h", b=2, c=2), sums_of(t)[:, :, :, P:VA],
                                      1e-8, None, ALU.add).then_inc(a_s, 1)
                eng.wait_ge(a_s, i * 3 + 2)
                eng.reciprocal(den[:, :, :], den[:, :, :]).then_inc(a_s, 1)
                eng.wait_ge(a_s, i * 3 + 3)
                if due(i):
                    eng.wait_ge(t_a, i)
                for t in range(T):
                    for b in range(2):
                        heads = den[:, t, b * 8:(b + 1) * 8].rearrange("p (c h) -> p c h", c=2)
                        ins = eng.tensor_tensor(
                            at[:, t, b * 2 * P:(b + 1) * 2 * P].rearrange("p (c h e) -> p c h e", c=2, h=HPB),
                            sums_of(t)[:, b, :, 0:P].rearrange("p c (h e) -> p c h e", h=HPB),
                            heads.unsqueeze(3).broadcast_to([P, 2, HPB, DK]), ALU.mult)
                ins.then_inc(a_r, 1)
                if tail:
                    weights(i - 1)
                choose(i, 0, (2, 3))
                eng.wait_ge(a_high, i + 1)
                if due(i):
                    eng.wait_ge(p_o, i)
                eng.tensor_tensor(al[:, :, :].rearrange("p k s -> p (k s)"), two(4).rearrange("p b s -> p (b s)"),
                                  ah[:, :, :].bitcast(F32).rearrange("p k s -> p (k s)"), ALU.subtract).then_inc(a_low, 1)
                bits(i, 1)
                choose(i, 1)
                if head:
                    bits(i + 1, 0)
                eng.wait_ge(p_o, i + 1)
                if due(i - 1):
                    eng.wait_ge(hb_r, i - 1)
                if due(i - 1):
                    eng.wait_ge(y_r, i - 1)
                eng.tensor_tensor(h1[:, p], two(6), bo[:, :].unsqueeze(1).broadcast_to([P, T, DM]), ALU.add).then_inc(h1_r, 1)

            low_of_weight(0)
            stats_h(0)
            low_of_weight(1)
            low_of_x(0)
            low_of_weight(2)
            low_of_weight(3)
            eng.wait_ge(w_low, 4)
            eng.wait_ge(c_in, 6 * 16)
            eng.wait_ge(const_s, 15)
            bits(0, 0)
            run(eng, step)
            stats_h1(NB - 1, 1)
            logits(NB - 1)
            ranks(NB - 1)
            taken(NB - 1)
            weights(NB - 1)

        @block.tensor
        def _(eng):
            def parts(j, k, cols):
                return WH[:, j, k, cols], WL[:, j, k, cols]

            def x_parts(k, cols):
                return xh[:, k, cols], xl[:, k, cols]

            def tokens_of_h(i, q, count):
                eng.wait_ge(h_in[q], count * HH * KB * 16)
                if due(i - 1):
                    eng.wait_ge(h1_r, i - 1)
                for t in range(T):
                    for k in range(KB):
                        ins = eng.transpose(PS[:, 6 + t, k * P:(k + 1) * P], hT[:, q, k, t * P:(t + 1) * P], ident[:, :])
                ins.then_inc(t_h, 1)

            def features(src, out):
                for t in range(T):
                    for k in range(KB):
                        ins = eng.transpose(PS[:, 4 + k // 2, k % 2 * SEQ + t * P:k % 2 * SEQ + (t + 1) * P],
                                            src[:, t, k * P:(k + 1) * P], ident[:, :])
                ins.then_inc(out, 1)

            def rows(i):
                eng.wait_ge(lg_r, i + 1)
                for t in range(T):
                    ins = eng.matmul(PS[:, 2, t * P:(t + 1) * P], lg[:, t:t + 1].broadcast_to([P, P]), ident[:, :],
                                     start=True, stop=True)
                ins.then_inc(p_row, 1)

            def gather(i):
                eng.wait_ge(oh_r, i + 1)
                eng.wait_ge(es_r, i + 1)
                for t in range(T):
                    eng.matmul(PS[:, 2, SEQ:SEQ + 2], es[:, t:t + 1].broadcast_to([P, P]), ones[:, 0:2],
                               start=(t == 0), stop=(t == T - 1))
                for k in range(KB):
                    for t in range(T):
                        ins = eng.matmul(PS[:, 3, k * TOPK:(k + 1) * TOPK], yn[:, t, k * P:(k + 1) * P], oh[:, t, :],
                                         start=(t == 0), stop=(t == T - 1))
                ins.then_inc(p_g, 1)

            def spread(i):
                eng.wait_ge(ow_r, i + 1)
                for t in range(T):
                    ins = eng.transpose(PS[0:TOPK, 2, t * P:(t + 1) * P], ow[:, t, :], ident[:, :])
                ins.then_inc(p_t, 1)

            def q_product(i):
                eng.wait_ge(x_low, i + 1)
                if due(i):
                    eng.wait_ge(a_r, i)
                for ob in range(KB):
                    out = PS[:, ob // 2, ob % 2 * SEQ:(ob % 2 + 1) * SEQ]
                    for k in range(KB):
                        ins = split_product(eng, out, parts(WQ, k, slice(ob * P, (ob + 1) * P)), x_parts(k, slice(0, SEQ)),
                                            k == 0, k == KB - 1)
                ins.then_inc(p_q, 1)

            def step(i, p, place, head=True, tail=True):
                hq, group = place
                if due(i - 1):
                    eng.wait_ge(pt_r, i - 1)
                if not tail:
                    eng.wait_ge(w_low, WK + 1)
                for t in range(T):
                    for k in range(KB):
                        ins = split_product(eng, PS[:, 2 + t, :], x_parts(k, slice(t * P, (t + 1) * P)),
                                            parts(WK, k, slice(0, DM)), k == 0, k == KB - 1)
                ins.then_inc(p_k, 1)
                if head:
                    tokens_of_h(i + 1, (hq + 1) % HSLOTS, group + 1 + (hq + 1) // HSLOTS)
                if due(i):
                    eng.wait_ge(a_low, i)
                if not tail:
                    eng.wait_ge(w_low, WV + 1)
                for t in range(T):
                    for k in range(KB):
                        ins = split_product(eng, PS[:, 4 + t, :], x_parts(k, slice(t * P, (t + 1) * P)),
                                            parts(WV, k, slice(0, DM)), k == 0, k == KB - 1)
                ins.then_inc(p_v, 1)
                eng.wait_ge(k_sum, i + 1)
                if tail:
                    rows(i - 1)
                eng.wait_ge(q_exp, i + 1)
                eng.wait_ge(k_r, i + 1)
                eng.wait_ge(v_r, i + 1)
                for b in range(KB):
                    for t in range(T):
                        ins = eng.matmul(sums_of(0)[:, b // 2, b % 2, :], kf[:, t, b * P:(b + 1) * P], va[:, t, b, :],
                                         start=(t == 0), stop=(t == T - 1))
                ins.then_inc(p_kv, 1)
                if head:
                    eng.wait_ge(xn_r, i + 2)
                    features(xn, t_x)
                eng.wait_ge(q_r, i + 1)
                eng.wait_ge(kv_r, i + 1)
                if not head:
                    if due(i):
                        eng.wait_ge(h1_r, i)
                for t in range(T):
                    for b in range(KB):
                        ins = eng.matmul(sums_of(t)[:, b // 2, b % 2, :], q[:, b, t * P:(t + 1) * P], kv[:, b, :],
                                         start=True, stop=True)
                ins.then_inc(p_a, 1)
                if tail:
                    gather(i - 1)
                if head:
                    eng.wait_ge(x_low, i + 2)
                eng.wait_ge(a_r, i + 1)
                features(at, t_a)
                if tail:
                    spread(i - 1)
                if head:
                    q_product(i + 1)
                eng.wait_ge(a_low, i + 1)
                if not tail:
                    eng.wait_ge(w_low, WO + 1)
                for t in range(T):
                    for k in range(KB):
                        split_product(eng, PS[:, 6 + t, :], (ah[:, k, t * P:(t + 1) * P], al[:, k, t * P:(t + 1) * P]),
                                      parts(WO, k, slice(0, DM)), k == 0, False, skip_group_check=True)
                    for k in range(KB):
                        ins = eng.matmul(PS[:, 6 + t, k * P:(k + 1) * P], hT[:, hq, k, t * P:(t + 1) * P], ident[:, :],
                                         start=False, stop=True, is_transpose=True, skip_group_check=True)
                ins.then_inc(p_o, 1)

            tokens_of_h(0, 0, 1)
            eng.wait_ge(xn_r, 1)
            features(xn, t_x)
            eng.wait_ge(w_low, WQ + 1)
            q_product(0)
            run(eng, step)
            eng.wait_ge(k_sum, NB)
            rows(NB - 1)
            gather(NB - 1)
            spread(NB - 1)


def routed_ffn_phase(nc, PS, d, C):
    ctx = ExitStack()
    with ctx:
        sb = lambda name, shape, dt=F32: ctx.enter_context(nc.sbuf_tensor("ff_" + name, shape, dt))
        sem = lambda name: ctx.enter_context(nc.semaphore("ff_" + name))
        NT = NB * TOPK
        SLOTS = 4
        fx = sb("fx", [P, KB, NT])
        b1 = sb("b1", [P, FB])
        b2 = sb("b2", [P, DM])
        w1 = sb("w1", [P, SLOTS, KB, P])
        w2 = sb("w2", [P, SLOTS, DM])
        g = sb("g", [P, 2, NT])
        ol = sb("ol", [P, NT // P, DM])
        ws = sb("ws", [P, 2, WSC])
        li = sb("li", [P, 2, WDC], I32)
        lm = sb("lm", [P, 4, WDC], I32)
        lx = sb("lx", [P, 2, NLUT // 2, WDC], I32)

        c_in = sem("c_in")
        w_in = [sem(f"w_in{q}") for q in range(SLOTS)]
        p_1 = sem("p_1")
        p_2 = sem("p_2")
        g_r = sem("g_r")
        o_r, o_out = sem("o_r"), sem("o_out")
        ws_in = [sem(f"ws_in{p}") for p in range(2)]
        ws_high, ws_low = sem("ws_high"), sem("ws_low")
        l_in = [sem(f"l_in{p}") for p in range(2)]
        l_s, l_used, l_r, l_out = sem("l_s"), sem("l_used"), sem("l_r"), sem("l_out")
        a_apart, v_apart, _ = C["apart"]

        block = ctx.enter_context(nc.Block())

        def run(eng, step):
            for q in range(SLOTS):
                step(q, q, 0)
            each_batch(eng, step, SLOTS, FB, SLOTS)

        @block.sync
        def _(eng):
            eng.dma_start(fx[:, :, :], d["fx"]).then_inc(c_in, 16)
            eng.dma_start(b1[:, :], d["b1"]).then_inc(c_in, 16)
            eng.dma_start(b2[:, :], d["b2"].unsqueeze(0).broadcast_to([P, DM])).then_inc(c_in, 16)

            def step(f, q, group):
                if due(f - SLOTS + 1):
                    eng.wait_ge(p_1, f - SLOTS + 1)
                eng.dma_start(w1[:, q], d["W1"][f]).then_inc(w_in[q], 16)
                if due(f - SLOTS + 1):
                    eng.wait_ge(p_2, f - SLOTS + 1)
                eng.dma_start(w2[:, q], d["W2"][f]).then_inc(w_in[q], 16)
            run(eng, step)
            eng.wait_ge(o_r, NT // P)
            eng.dma_start(d["ol"].rearrange("(g p) d -> p g d", p=P), ol[:, :, :]).then_inc(o_out, 16)
            eng.wait_ge(o_out, 16)

        @block.gpsimd
        def _(eng):

            def step(f, q, group):
                p, pair = q % 2, group * 2 + q // 2
                if due(f - 1):
                    eng.wait_ge(l_used, f - 1)
                eng.dma_start(li[:, p], d["idx"][:, bass.ds(WD + f * WDC, WDC)]).then_inc(l_in[p], 16)
                if due(f - 1):
                    eng.wait_ge(ws_low, f - 1)
                eng.dma_start(ws[:, p], d["w"][:, bass.ds(f * WSC, WSC)].bitcast(F32)).then_inc(ws_in[p], 16)
            run(eng, step)

        @block.scalar
        def _(eng):
            eng.wait_ge(c_in, 48)

            def down_columns(f, p):
                eng.wait_ge(l_r, f + 1)
                eng.sem_inc(a_apart, 1)
                eng.activation(C["wd"][:, bass.ds(f * WDC, WDC)], lx[:, p, 0, :].bitcast(F32), ACT.Copy).then_inc(l_out, 1)

            def step(f, q, group):
                p, pair = q % 2, group * 2 + q // 2
                eng.wait_ge(ws_in[p], (pair + 1) * 16)
                eng.sem_inc(a_apart, 1)
                eng.activation(C["wgh"][:, bass.ds(f * WSC, WSC)], ws[:, p], ACT.Copy).then_inc(ws_high, 1)
                if due(f - 1):
                    eng.wait_ge(p_2, f - 1)
                eng.wait_ge(p_1, f + 1)
                eng.sem_inc(a_apart, 1)
                eng.activation(g[:, p, :], PS[:, 4 + p, :], ACT.Gelu, bias=b1[:, bass.ds(f, 1)]).then_inc(g_r, 1)
                if due(f):
                    down_columns(f - 1, 1 - p)
            run(eng, step)
            down_columns(FB - 1, 1)

        @block.vector
        def _(eng):
            def step(f, q, group):
                p, pair = q % 2, group * 2 + q // 2
                eng.wait_ge(l_in[p], (pair + 1) * 16)
                if due(f - 1):
                    eng.wait_ge(l_out, f - 1)
                if due(f):
                    eng.wait_ge(l_r, f)
                table_bits(eng, li[:, p, :], lm, lx[:, p], C["pairs"], C["lut"], l_s, l_used, f)
                table_choice(eng, lm, lx[:, p], WDC, l_s, l_used, f, l_r, v_apart)
                eng.wait_ge(ws_high, f + 1)
                eng.sem_inc(v_apart, 1)
                eng.tensor_tensor(C["wgl"][:, bass.ds(f * WSC, WSC)], ws[:, p],
                                  C["wgh"][:, bass.ds(f * WSC, WSC)].bitcast(F32), ALU.subtract).then_inc(ws_low, 1)
            run(eng, step)
            eng.wait_ge(p_2, FB)
            eng.wait_ge(c_in, 48)
            for t in range(NT // P):
                eng.tensor_tensor(ol[:, t, :], PS[:, t, :], b2[:, :], ALU.add).then_inc(o_r, 1)

        @block.tensor
        def _(eng):
            def first(f, q, group):
                eng.wait_ge(w_in[q], (group + 1) * 32)
                if due(f - 1):
                    eng.wait_ge(g_r, f - 1)
                for k in range(KB):
                    ins = eng.matmul(PS[:, 4 + q % 2, :], w1[:, q, k, :], fx[:, k, :], start=(k == 0), stop=(k == KB - 1))
                ins.then_inc(p_1, 1)

            def second(f, q, group, start=False, stop=False):
                eng.wait_ge(w_in[q], (group + 1) * 32)
                eng.wait_ge(g_r, f + 1)
                for t in range(NT // P):
                    ins = eng.matmul(PS[:, t, :], g[:, q % 2, t * P:(t + 1) * P], w2[:, q, :], start=start, stop=stop)
                ins.then_inc(p_2, 1)

            def step(f, q, group):
                first(f, q, group)
                second(f - 1, (q - 1) % SLOTS, group if q else group - 1)
            eng.wait_ge(c_in, 48)
            first(0, 0, 0)
            first(1, 1, 0)
            second(0, 0, 0, start=True)
            for q in range(2, SLOTS):
                step(q, q, 0)
            each_batch(eng, step, SLOTS, FB, SLOTS)
            second(FB - 1, SLOTS - 1, FB // SLOTS - 1, stop=True)


def scan_phase(nc, PS, d, C):
    ctx = ExitStack()
    with ctx:
        sb = lambda name, shape, dt=F32: ctx.enter_context(nc.sbuf_tensor("sc_" + name, shape, dt))
        sem = lambda name: ctx.enter_context(nc.semaphore("sc_" + name))
        ident, halves, wgh, wgl, wd = C["ident"], C["halves"], C["wgh"], C["wgl"], C["wd"]
        BCR = 2 * SS
        sel = sb("sel", [3 * BCR, BCR], BF16)
        wp = sb("wp", [P, KB, DTR + 3 * BCR])
        right = sb("right", [DTR + TOPK, DM])
        wdo = right[0:DTR]
        ol = right[DTR:DTR + TOPK]
        left = sb("left", [DTR + TOPK, SEQ])
        dtr = left[0:DTR]
        pt = left[DTR:DTR + TOPK]
        bdt = sb("bdt", [P, KB])
        Dc = sb("Dc", [P, KB])
        al = sb("al", [P, KB, SS])
        A = sb("A", [P, KB, SS])
        h2 = sb("h2", [P, 2, T, DM])
        stz = sb("stz", [P, T, 6])
        mvz = sb("mvz", [P, T, 2])
        vez = sb("vez", [P, T])
        rsz = sb("rsz", [P, T])
        nmz = sb("nmz", [P, T])
        xn = sb("xn", [P, T, DM])
        zT = sb("zT", [P, KB, SEQ])
        diag = sb("diag", [P, KB, P])
        b1 = sb("b1", [3 * BCR, SEQ])
        bc = sb("bc", [3 * BCR, 2, SEQ], BF16)
        dt = sb("dt", [P, 2, KB, SEQ])
        du = sb("du", [P, 2, KB, SEQ])
        bs = sb("bs", [P, 2, SEQ])
        a = sb("a", [P, 2, KB, SEQ])
        bu = sb("bu", [P, 2, KB, SEQ])
        cx = sb("cx", [P, 2, KB, SEQ])
        h3 = sb("h3", [P, 2, T, DM])
        stf = sb("stf", [P, T, 6])
        mvf = sb("mvf", [P, T, 2])
        vef = sb("vef", [P, T])
        rsf = sb("rsf", [P, T])
        nmf = sb("nmf", [P, T])
        fh = sb("fh", [P, KB, SEQ], F32R)
        fl = sb("fl", [P, KB, SEQ], F32R)
        th = sb("th", [P, 2, SEQ])
        hh = sb("hh", [P, IB, SEQ])

        c_in, c_s, c_a = sem("c_in"), sem("c_s"), sem("c_a")
        f_in = sem("f_in")
        p_sc, h2_r, stz_s, mvz_r, rootz_s, rsz_r, zn_r, t_z, z_r = (
            sem(n) for n in ("p_sc", "h2_r", "stz_s", "mvz_r", "rootz_s", "rsz_r", "zn_r", "t_z", "z_r"))
        p_pj, dtr_r, bc_s, bc_r, p_dt, xb_r, ax_r, sp_s, sp_r, dt_s, du_r, dt_r = (
            sem(n) for n in ("p_pj", "dtr_r", "bc_s", "bc_r", "p_dt", "xb_r", "ax_r", "sp_s", "sp_r", "dt_s", "du_r", "dt_r"))
        b_r, p_bc, a_r, bu_s, scan_s, cx_s, p_zd, y_s = (sem(n) for n in ("b_r", "p_bc", "a_r", "bu_s", "scan_s", "cx_s", "p_zd", "y_s"))
        h3_r, stf_s, mvf_r, rootf_s, rsf_r, fn_r, t_f, f_h, f_r = (
            sem(n) for n in ("h3_r", "stf_s", "mvf_r", "rootf_s", "rsf_r", "fn_r", "t_f", "f_h", "f_r"))
        p_gu, th_r, m_s, hh_r, p_dn, h4_r, s_out = (sem(n) for n in ("p_gu", "th_r", "m_s", "hh_r", "p_dn", "h4_r", "s_out"))
        _, v_apart, g_apart = C["apart"]

        YB, MB, CB, GB = 0, 2, 4, 6
        two = lambda b: PS[:, b:b + 2, :]
        GATE = SS - IB
        rows_of = lambda k: P if k < IB - 1 else ILAST
        DOWN = {0: (0, 1, 2), 1: (3, 4), 2: (5, 6, 7), 3: (8, 9, 10)}
        flat = lambda x: x.rearrange("p k s -> p (k s)")
        by_tile = lambda x: x[:, :, :].rearrange("p k (t s) -> p t k s", t=T)
        by_tile_of = lambda b: PS[:, b:b + T, :].rearrange("p t (k s) -> p t k s", k=KB)

        def run(eng, step):
            step(0, 0, 0, back=False, down=False)
            step(1, 1, 0, down=False)
            step(2, 0, 1)
            step(3, 1, 1)
            each_batch(eng, step, 4, NB - 2)
            step(NB - 2, 0, NB // 2 - 1)
            step(NB - 1, 1, NB // 2 - 1, front=False)
            step(NB, 0, NB // 2, front=False, mid=False)
            step(NB + 1, 1, NB // 2, front=False, mid=False, back=False)

        block = ctx.enter_context(nc.Block())

        @block.sync
        def _(eng):
            def load_constants():
                eng.dma_start(wp[:, :, 0:DTR], d["w_dti"]).then_inc(c_in, 16)
                for g in range(3):
                    at = DTR + g * BCR
                    eng.dma_start(wp[:, :, at:at + BCR], d["w_bc"]).then_inc(c_in, 16)
                eng.dma_start(wdo[:, :], d["w_dto"]).then_inc(c_in, 16)
                for tile, name in ((bdt, "b_dt"), (Dc, "D"), ):
                    eng.dma_start(tile[:, :], d[name]).then_inc(c_in, 16)
                eng.dma_start(al[:, :, :], d["A_log"]).then_inc(c_in, 16)

            def load(b, p):
                if due(b):
                    eng.wait_ge(h2_r, b)
                if due(b - 1):
                    eng.wait_ge(h3_r, b - 1)
                eng.dma_start(h2[:, p].rearrange("p t d -> p (t d)"), d["hb"][b]).then_inc(f_in, 16)
                eng.dma_start(ol[:, :], d["ol"][bass.ds(b * TOPK, TOPK), :]).then_inc(f_in, 16)
                eng.dma_start(pt[:, :], d["pt"][:, bass.ds(b * SEQ, SEQ)]).then_inc(f_in, 16)

            def store(b, p):
                eng.wait_ge(h4_r, b + 1)
                eng.dma_start(d["out"].rearrange("b (t p) d -> b p t d", p=P)[b], h3[:, p]).then_inc(s_out, 16)

            def step(i, p, pair, front=True, mid=True, back=True, down=True):
                if front:
                    load(i + 1, 1 - p)
                if down:
                    store(i - 2, p)
            load(0, 0)
            load_constants()
            run(eng, step)
            eng.wait_ge(s_out, NB * 16)

        @block.gpsimd
        def _(eng):
            eng.memset(sel[:, :], 0.0).then_inc(c_s, 1)
            for g in range(3):
                eng.wait_ge(c_s, g + 1)
                eng.affine_select(out=sel[:, :], in_=sel[:, :], compare_op=ALU.not_equal, fill=1.0,
                                  base=-g * BCR, pattern=[[-1, BCR]], channel_multiplier=1).then_inc(c_s, 1)

            def root_z(b):
                inverse_root(eng, b + 1, mvz_r, mvz, vez[:, :], rsz[:, :], nmz[:, :], halves, zn_r, rootz_s, b, rsz_r, g_apart)

            def root_f(b):
                inverse_root(eng, b + 1, mvf_r, mvf, vef[:, :], rsf[:, :], nmf[:, :], halves, fn_r, rootf_s, b, rsf_r, g_apart)

            def inputs(b, p, n):
                m = b * SS + n
                eng.wait_ge(du_r, b + 1)
                eng.wait_ge(b_r, m + 1)
                if due(m - 1):
                    eng.wait_ge(cx_s, m - 1)
                eng.tensor_tensor(bu[:, n % 2], du[:, p], bs[:, n % 2, :].unsqueeze(1).broadcast_to([P, KB, SEQ]),
                                  ALU.mult).then_inc(bu_s, 1)

            def step(i, p, pair, front=True, mid=True, back=True, down=True):
                for n in range(SS):
                    if back and n == 2:
                        root_f(i - 1)
                    if front and n == 7:
                        root_z(i + 1)
                    if mid and n + 1 < SS:
                        inputs(i, p, n + 1)
                    if front and n + 1 == SS:
                        inputs(i + 1, 1 - p, 0)
            root_z(0)
            inputs(0, 0, 0)
            run(eng, step)

        @block.scalar
        def _(eng):
            def normalise_z(b, p):
                eng.wait_ge(rsz_r, b + 1)
                if due(b - 1):
                    eng.wait_ge(t_f, b - 1)
                for t in range(T):
                    ins = eng.activation(xn[:, t, :], h2[:, p, t, :], ACT.Identity, bias=nmz[:, t:t + 1], scale=rsz[:, t:t + 1])
                ins.then_inc(zn_r, 1)

            def transposed_z(b):
                eng.wait_ge(t_z, b + 1)
                if due(b):
                    eng.wait_ge(p_pj, b)
                if due(b):
                    eng.wait_ge(du_r, b)
                if due(b):
                    eng.wait_ge(p_zd, b)
                for t in range(T):
                    ins = eng.activation(zT[:, :, t * P:(t + 1) * P], PS[:, MB + t, :].rearrange("p (k s) -> p k s", k=KB), ACT.Copy)
                ins.then_inc(z_r, 1)

            def rank_input(b):
                eng.wait_ge(p_pj, b + 1)
                if due(b):
                    eng.wait_ge(p_dt, b)
                eng.activation(dtr[:, :], PS[0:DTR, MB, 0:SEQ], ACT.Copy).then_inc(dtr_r, 1)

            def softplus(b, p):
                eng.wait_ge(ax_r, b + 1)
                eng.activation(flat(dt[:, p]), flat(dt[:, p]), ACT.Exp).then_inc(sp_s, 1)
                eng.wait_ge(sp_s, b + 1)
                eng.activation(flat(dt[:, p]), flat(dt[:, p]), ACT.Ln, bias=1.0).then_inc(sp_r, 1)

            def everywhere(b, n):
                m = b * SS + n
                eng.wait_ge(p_bc, m + 1)
                if due(m - 1):
                    eng.wait_ge(bu_s, m - 1)
                eng.activation(bs[:, n % 2, :], PS[:, CB + n % 2, 0:SEQ], ACT.Copy).then_inc(b_r, 1)

            def decay(b, p, n):
                m = b * SS + n
                eng.wait_ge(dt_r, b + 1)
                if due(m - 1):
                    eng.wait_ge(scan_s, m - 1)
                for k in range(KB):
                    ins = eng.activation(a[:, n % 2, k, :], dt[:, p, k, :], ACT.Exp, scale=A[:, k, n:n + 1])
                ins.then_inc(a_r, 1)

            def normalise_f(b, p):
                eng.wait_ge(rsf_r, b + 1)
                eng.wait_ge(t_z, min(b + 2, NB) if isinstance(b, int) else b + 2)
                for t in range(T):
                    ins = eng.activation(xn[:, t, :], h3[:, p, t, :], ACT.Identity, bias=nmf[:, t:t + 1], scale=rsf[:, t:t + 1])
                ins.then_inc(fn_r, 1)

            def transposed_f(b):
                eng.wait_ge(t_f, b + 1)
                if due(b * IB):
                    eng.wait_ge(p_gu, b * IB)
                eng.activation(by_tile(fh), by_tile_of(MB), ACT.Copy).then_inc(f_h, 1)

            def tanh(b, k):
                m = rows_of(k)
                eng.wait_ge(p_gu, b * IB + k + 1)
                if due(b * IB + k - (1 if k else 0)):
                    eng.wait_ge(hh_r, b * IB + k - (1 if k else 0))
                eng.activation(th[0:m, k % 2, :], PS[0:m, GB + k % 2, 0:SEQ], ACT.Tanh, scale=0.5).then_inc(th_r, 1)

            def step(i, p, pair, front=True, mid=True, back=True, down=True):
                for n in range(SS):
                    if mid and n + 1 < SS:
                        everywhere(i, n + 1)
                        decay(i, p, n + 1)
                    if front and n + 1 == SS:
                        everywhere(i + 1, 0)
                        decay(i + 1, 1 - p, 0)
                    if back and n == 2:
                        normalise_f(i - 1, 1 - p)
                    if back and n == 3:
                        transposed_f(i - 1)
                    if back and n >= GATE:
                        tanh(i - 1, n - GATE)
                    if front and n == 7:
                        normalise_z(i + 1, 1 - p)
                    if front and n == 8:
                        transposed_z(i + 1)
                    if front and n == 10:
                        rank_input(i + 1)
                    if front and n == 12:
                        softplus(i + 1, 1 - p)

            normalise_z(0, 0)
            transposed_z(0)
            eng.wait_ge(c_in, 8 * 16)
            eng.activation(A[:, :, :], al[:, :, :], ACT.Exp).then_inc(c_a, 1)
            rank_input(0)
            softplus(0, 0)
            everywhere(0, 0)
            eng.wait_ge(c_a, 3)
            decay(0, 0, 0)
            run(eng, step)

        @block.vector
        def _(eng):
            def residual_z(b, p):
                eng.wait_ge(p_sc, b + 1)
                eng.tensor_tensor(h2[:, p], two(MB), h2[:, p], ALU.add).then_inc(h2_r, 1)

            def statistics_z(b, p):
                eng.wait_ge(h2_r, b + 1)
                if due(b):
                    eng.wait_ge(rsz_r, b)
                statistics(eng, [h2[:, p, t, :] for t in range(T)], stz, mvz, stz_s, b, mvz_r, v_apart)

            def parts(b, p):
                eng.wait_ge(p_pj, b + 1)
                if due((b - 1) * SS):
                    eng.wait_ge(p_bc, (b - 1) * SS)
                if due(b):
                    eng.wait_ge(bc_r, b)
                src = PS[0:3 * BCR, MB + 1, 0:SEQ]
                r = [slice(g * BCR, (g + 1) * BCR) for g in range(3)]
                eng.tensor_copy(bc[:, p, :], src).then_inc(bc_s, 1)
                eng.wait_ge(bc_s, b * 4 + 1)
                eng.tensor_tensor(b1[:, :], src, bc[:, p, :], ALU.subtract).then_inc(bc_s, 1)
                eng.wait_ge(bc_s, b * 4 + 2)
                eng.tensor_copy(bc[r[1], p, :], b1[r[1], :]).then_inc(bc_s, 1)
                eng.tensor_copy(bc[r[2], p, :], b1[r[2], :]).then_inc(bc_s, 1)
                eng.wait_ge(bc_s, b * 4 + 4)
                eng.tensor_tensor(bc[r[2], p, :], b1[r[2], :], bc[r[2], p, :], ALU.subtract).then_inc(bc_r, 1)

            def raw_dt(b, p):
                eng.wait_ge(p_dt, b + 1)
                if due((b - 1) * SS):
                    eng.wait_ge(bu_s, (b - 1) * SS)
                eng.tensor_tensor(du[:, p].rearrange("p (b c) s -> p b c s", c=2), two(MB).rearrange("p b (c s) -> p b c s", c=2),
                                  bdt[:, :].rearrange("p (b c) -> p b c", c=2).unsqueeze(3).broadcast_to([P, 2, 2, SEQ]),
                                  ALU.add).then_inc(xb_r, 1)
                eng.wait_ge(xb_r, b + 1)
                if due((b - 1) * SS):
                    eng.wait_ge(a_r, (b - 1) * SS)
                eng.scalar_tensor_tensor(out=flat(dt[:, p]), in0=flat(du[:, p]), scalar=-1.0, in1=flat(du[:, p]),
                                         op0=ALU.mult, op1=ALU.min).then_inc(ax_r, 1)

            def make_dt(b, p):
                eng.wait_ge(sp_r, b + 1)
                eng.scalar_tensor_tensor(out=flat(dt[:, p]), in0=flat(du[:, p]), scalar=0.0, in1=flat(dt[:, p]),
                                         op0=ALU.max, op1=ALU.add).then_inc(dt_s, 1)

            def make_du(b, p):
                eng.wait_ge(dt_s, b + 1)
                eng.tensor_tensor(flat(du[:, p]), flat(dt[:, p]), flat(zT[:, :, :]), ALU.mult).then_inc(du_r, 1)
                eng.wait_ge(du_r, b + 1)
                eng.memset(dt[:, p, :, 0:1], 1e30).then_inc(dt_r, 1)

            def scan(b, n):
                m = b * SS + n
                eng.wait_ge(a_r, m + 1)
                eng.wait_ge(bu_s, m + 1)
                if due(m):
                    eng.wait_ge(cx_s, m)
                eng.tensor_tensor_scan(flat(bu[:, n % 2]), flat(a[:, n % 2]), flat(bu[:, n % 2]), 0.0, ALU.mult, ALU.add).then_inc(scan_s, 1)

            def outputs(b, n):
                m = b * SS + n
                eng.wait_ge(scan_s, m + 1)
                if due(m - 1):
                    eng.wait_ge(y_s, m - 1)
                eng.tensor_tensor(cx[:, n % 2], bu[:, n % 2], PS[:, CB + n % 2, SEQ:2 * SEQ].unsqueeze(1).broadcast_to([P, KB, SEQ]),
                                  ALU.mult).then_inc(cx_s, 1)

            def residual_f(b, p):
                eng.wait_ge(y_s, (b + 1) * SS)
                if due((b - 1) * 16):
                    eng.wait_ge(s_out, (b - 1) * 16)
                eng.tensor_tensor(h3[:, p], two(YB), h2[:, p], ALU.add).then_inc(h3_r, 1)

            def statistics_f(b, p):
                eng.wait_ge(h3_r, b + 1)
                if due(b):
                    eng.wait_ge(rsf_r, b)
                statistics(eng, [h3[:, p, t, :] for t in range(T)], stf, mvf, stf_s, b, mvf_r, v_apart)

            def low_f(b):
                eng.wait_ge(f_h, b + 1)
                if due(b * IB):
                    eng.wait_ge(p_gu, b * IB)
                eng.tensor_tensor(by_tile(fl), by_tile_of(MB), by_tile(fh).bitcast(F32), ALU.subtract).then_inc(f_r, 1)

            def gated(b, k):
                m, at = rows_of(k), b * IB + k
                eng.wait_ge(th_r, at + 1)
                if due(at):
                    eng.wait_ge(hh_r, at)
                eng.scalar_tensor_tensor(out=th[0:m, k % 2, :], in0=th[0:m, k % 2, :], scalar=1.0, in1=PS[0:m, GB + k % 2, 0:SEQ],
                                         op0=ALU.add, op1=ALU.mult).then_inc(m_s, 1)
                eng.wait_ge(m_s, at + 1)
                if due(b):
                    eng.wait_ge(p_dn, b)
                eng.scalar_tensor_tensor(out=hh[0:m, k, :], in0=th[0:m, k % 2, :], scalar=0.5, in1=PS[0:m, GB + k % 2, SEQ:2 * SEQ],
                                         op0=ALU.mult, op1=ALU.mult).then_inc(hh_r, 1)

            def final(b, p):
                eng.wait_ge(p_dn, b + 1)
                eng.tensor_tensor(h3[:, p], two(GB), h3[:, p], ALU.add).then_inc(h4_r, 1)

            def step(i, p, pair, front=True, mid=True, back=True, down=True):
                for n in range(SS):
                    if mid:
                        scan(i, n)
                    if back and n == 0:
                        residual_f(i - 1, 1 - p)
                    if mid:
                        outputs(i, n)
                    if back and n == 1:
                        statistics_f(i - 1, 1 - p)
                    if down and n == 4:
                        final(i - 2, p)
                    if back and n == 4:
                        low_f(i - 1)
                    if back and n >= GATE:
                        gated(i - 1, n - GATE)
                    if front and n == 5:
                        residual_z(i + 1, 1 - p)
                    if front and n == 6:
                        statistics_z(i + 1, 1 - p)
                    if front and n == 10:
                        parts(i + 1, 1 - p)
                    if front and n == 11:
                        raw_dt(i + 1, 1 - p)
                    if front and n == 13:
                        make_dt(i + 1, 1 - p)
                    if front and n == 14:
                        make_du(i + 1, 1 - p)

            residual_z(0, 0)
            statistics_z(0, 0)
            eng.wait_ge(c_in, 8 * 16)
            for k in range(KB):
                ins = eng.tensor_scalar(diag[:, k, :], ident[:, :], Dc[:, k:k + 1], None, ALU.mult)
            ins.then_inc(c_a, 1)
            eng.wait_ge(c_a, 2)
            eng.tensor_scalar(A[:, :, :], A[:, :, :], -1.0, None, ALU.mult).then_inc(c_a, 1)
            parts(0, 0)
            raw_dt(0, 0)
            make_dt(0, 0)
            make_du(0, 0)
            run(eng, step)

        @block.tensor
        def _(eng):
            def scatter(b):
                eng.wait_ge(f_in, (b + 1) * 48)
                if due(b):
                    eng.wait_ge(xb_r, b)
                if due(b - 1):
                    eng.wait_ge(f_r, b - 1)
                for t in range(T):
                    ins = eng.matmul(PS[:, MB + t, :], pt[:, t * P:(t + 1) * P], ol[:, :], start=True, stop=True)
                ins.then_inc(p_sc, 1)

            def features(src, out):
                for t in range(T):
                    for k in range(KB):
                        ins = eng.transpose(PS[:, MB + t, k * P:(k + 1) * P], src[:, t, k * P:(k + 1) * P], ident[:, :])
                ins.then_inc(out, 1)

            def features_z(b):
                eng.wait_ge(zn_r, b + 1)
                eng.wait_ge(h2_r, b + 1)
                features(xn, t_z)

            def projections(b):
                eng.wait_ge(z_r, b + 1)
                for k in range(KB):
                    eng.matmul(PS[0:DTR, MB, 0:SEQ], wp[:, k, 0:DTR], zT[:, k, :], start=(k == 0), stop=(k == KB - 1))
                for k in range(KB):
                    ins = eng.matmul(PS[0:3 * BCR, MB + 1, 0:SEQ], wp[:, k, DTR:DTR + 3 * BCR], zT[:, k, :],
                                     start=(k == 0), stop=(k == KB - 1))
                ins.then_inc(p_pj, 1)

            def dt_product(b):
                eng.wait_ge(dtr_r, b + 1)
                eng.wait_ge(bc_r, b + 1)
                for k in range(KB):
                    ins = eng.matmul(PS[:, MB + k // 2, k % 2 * SEQ:(k % 2 + 1) * SEQ], wdo[:, k * P:(k + 1) * P], dtr[:, :],
                                     start=True, stop=True)
                ins.then_inc(p_dt, 1)

            def broadcasts(b, p, n):
                m = b * SS + n
                eng.wait_ge(bc_r, b + 1)
                if due(m - 1):
                    eng.wait_ge(cx_s, m - 1)
                for j in range(2):
                    ins = eng.matmul(PS[:, CB + n % 2, j * SEQ:(j + 1) * SEQ], sel[:, j * SS + n:j * SS + n + 1].broadcast_to([3 * BCR, P]), bc[:, p, :], start=True, stop=True)
                ins.then_inc(p_bc, 1)

            def output(b, n):
                m = b * SS + n
                if n == 0:
                    if due(b):
                        eng.wait_ge(h3_r, b)
                    eng.wait_ge(z_r, b + 1)
                    for t in range(T):
                        for k in range(KB):
                            ins = eng.matmul(PS[:, YB + t, k * P:(k + 1) * P], zT[:, k, t * P:(t + 1) * P], diag[:, k, :],
                                             start=(k == 0), stop=False, skip_group_check=True)
                    ins.then_inc(p_zd, 1)
                eng.wait_ge(cx_s, m + 1)
                for t in range(T):
                    for k in range(KB):
                        ins = eng.matmul(PS[:, YB + t, k * P:(k + 1) * P], cx[:, n % 2, k, t * P:(t + 1) * P], ident[:, :],
                                         start=False, stop=(n == SS - 1), is_transpose=True, skip_group_check=True)
                ins.then_inc(y_s, 1)

            def features_f(b):
                eng.wait_ge(fn_r, b + 1)
                eng.wait_ge(xb_r, min(b + 2, NB) if isinstance(b, int) else b + 2)
                features(xn, t_f)

            def gate_up(b, k):
                at, m = b * IB + k, rows_of(k)
                eng.wait_ge(f_r, b + 1)
                if k < 2:
                    if due(b):
                        eng.wait_ge(h4_r, b)
                else:
                    if due(at - 1):
                        eng.wait_ge(hh_r, at - 1)
                for j, base in enumerate((WG, WU)):
                    for kb in range(KB):
                        at_w = base + kb * INTER + k * P
                        ins = split_product(eng, PS[0:m, GB + k % 2, j * SEQ:(j + 1) * SEQ],
                                            (wgh[:, at_w:at_w + m], wgl[:, at_w:at_w + m]), (fh[:, kb, :], fl[:, kb, :]),
                                            kb == 0, kb == KB - 1)
                ins.then_inc(p_gu, 1)

            def down_product(b, blocks):
                eng.wait_ge(hh_r, (b + 1) * IB)
                for k in blocks:
                    m = rows_of(k)
                    for t in range(T):
                        ins = eng.matmul(PS[:, GB + t, :], hh[0:m, k, t * P:(t + 1) * P], wd[0:m, k * DM:(k + 1) * DM],
                                         start=(k == 0), stop=(k == IB - 1))
                if blocks[-1] == IB - 1:
                    ins.then_inc(p_dn, 1)

            def step(i, p, pair, front=True, mid=True, back=True, down=True):
                for n in range(SS):
                    if n == 0 and back:
                        output(i - 1, SS - 1)
                    if mid and n > 0:
                        output(i, n - 1)
                    if back and n == 3:
                        features_f(i - 1)
                    if down and n in DOWN:
                        down_product(i - 2, DOWN[n])
                    if back and n >= GATE:
                        gate_up(i - 1, n - GATE)
                    if front and n == 5:
                        scatter(i + 1)
                    if front and n == 8:
                        features_z(i + 1)
                    if front and n == 10:
                        projections(i + 1)
                    if front and n == 11:
                        dt_product(i + 1)
                    if mid and n + 2 < SS:
                        broadcasts(i, p, n + 2)
                    if front and n + 2 >= SS:
                        broadcasts(i + 1, 1 - p, n + 2 - SS)

            scatter(0)
            features_z(0)
            eng.wait_ge(c_in, 8 * 16)
            projections(0)
            dt_product(0)
            eng.wait_ge(c_s, 4)
            eng.wait_ge(c_a, 2)
            broadcasts(0, 0, 0)
            broadcasts(0, 0, 1)
            run(eng, step)


def build(nc, d):
    for name, shape, dt in (("hT", [NCH, P, LC * HH * HC], F32), ("hb", [NB, P, T * DM], F32), ("fx", [P, KB, NB * TOPK], F32),
                            ("pt", [TOPK, NB * SEQ], F32), ("ol", [NB * TOPK, DM], F32), ("w", [P, WD], I32)):
        if name not in d:
            d[name] = nc.dram_tensor("scratch_" + name, shape, dt, kind="Internal").ap()
    ctx = ExitStack()
    with ctx:
        PS = ctx.enter_context(nc.psum_tensor("PS", [P, 8, 512], F32))
        ident = ctx.enter_context(nc.sbuf_tensor("ident", [P, P], F32))
        halves = ctx.enter_context(nc.sbuf_tensor("halves", [P, T], F32))
        lut = ctx.enter_context(nc.sbuf_tensor("lut_sb", [P, NLUT], I32))
        pairs = ctx.enter_context(nc.sbuf_tensor("pairs", [P, NLUT // 2], I32))
        made = ctx.enter_context(nc.semaphore("constants_made"))
        loaded = ctx.enter_context(nc.semaphore("table_loaded"))
        apart = [ctx.enter_context(nc.semaphore("apart_" + e)) for e in ("scalar", "vector", "gpsimd")]
        C = {"ident": ident, "halves": halves, "lut": lut, "pairs": pairs, "apart": apart}
        with nc.Block() as block:
            @block.sync
            def _(eng):
                eng.dma_start(lut[:, :].bitcast(F32), d["lut"].unsqueeze(0).broadcast_to([P, NLUT])).then_inc(loaded, 16)
                eng.wait_ge(loaded, 16)

            @block.vector
            def _(eng):
                eng.wait_ge(loaded, 16)
                eng.tensor_tensor(pairs[:, :], lut[:, 0:NLUT:2], lut[:, 1:NLUT:2], ALU.bitwise_xor).then_inc(made, 1)

            @block.gpsimd
            def _(eng):
                eng.memset(halves[:, :], -0.5).then_inc(made, 1)
                eng.memset(ident[:, :], 0.0).then_inc(made, 1)
                eng.wait_ge(made, 3)
                eng.affine_select(out=ident[:, :], in_=ident[:, :], compare_op=ALU.not_equal, fill=1.0, base=0,
                                  pattern=[[-1, P]], channel_multiplier=1).then_inc(made, 1)
                eng.wait_ge(made, 4)
        s4d_phase(nc, PS, d)
        attention_phase(nc, PS, d, C)
        C["wgh"] = ctx.enter_context(nc.sbuf_tensor("wgh", [P, WD], F32R))
        C["wgl"] = ctx.enter_context(nc.sbuf_tensor("wgl", [P, WD], F32R))
        C["wd"] = ctx.enter_context(nc.sbuf_tensor("wd", [P, IB * DM], F32))
        routed_ffn_phase(nc, PS, d, C)
        scan_phase(nc, PS, d, C)


def kernel(**inputs):
    import concourse.bacc as bacc
    from concourse.bass_utils import run_bass_kernel_spmd

    x = {k: np.asarray(v) for k, v in inputs.items()}

    def by_state(a):
        return a.reshape(HH, P, NSTATE).transpose(0, 2, 1).reshape(HH * NSTATE, P)

    def by_input(w):
        return w.reshape(KB, P, -1).transpose(1, 0, 2)

    columns = lambda v: v.reshape(KB, P).T
    index = [by_input(x[f"L1_ffn_{n}_idx"].T).reshape(P, -1) for n in ("gate", "up")]
    down = np.zeros((IB * P, DM), np.int32)
    down[:INTER] = x["L1_ffn_down_idx"].T
    index.append(down.reshape(IB, P, DM).transpose(1, 0, 2).reshape(P, -1))
    arrays = {
        "xc": x["x"].reshape(NB, HH, P, NSTATE, 2).transpose(1, 3, 4, 2, 0).reshape(P, 2, P, NB),
        "log_dt": x["L0_tok_log_dt"],
        "inv_A_real": by_state(x["L0_tok_inv_A_real"]), "A_imag": by_state(x["L0_tok_A_imag"]),
        "B_re": by_state(x["L0_tok_B_ri"][..., 0]), "B_im": by_state(x["L0_tok_B_ri"][..., 1]),
        "w_attn": np.stack([by_input(x["L0_attn_" + n].T) for n in ("wq", "wk", "wv", "wo")]),
        "bq": columns(x["L0_attn_bq"]), "bk": x["L0_attn_bk"], "bv": x["L0_attn_bv"], "bo": x["L0_attn_bo"],
        "Wr": x["L0_ffn_Wr"].reshape(DM), "br": x["L0_ffn_br"],
        "W1": x["L0_ffn_W1"].reshape(KB, P, FB, P).transpose(2, 1, 0, 3), "b1": x["L0_ffn_b1"].reshape(FB, P).T,
        "W2": x["L0_ffn_W2"].reshape(FB, P, DM), "b2": x["L0_ffn_b2"],
        "w_dti": by_input(x["L1_attn_W_dt_in"].T),
        "w_bc": by_input(np.concatenate([x["L1_attn_W_B"], x["L1_attn_W_C"]]).T),
        "w_dto": x["L1_attn_W_dt_out"].T, "b_dt": columns(x["L1_attn_b_dt_out"]), "D": columns(x["L1_attn_D"]),
        "A_log": by_input(x["L1_attn_A_log"]),
        "lut": x["L1_ffn_lut"], "idx": np.concatenate(index, 1),
    }
    nc = bacc.Bacc("TRN2", target_bir_lowering=False, num_devices=1)
    feed, d = {}, {}
    for name, a in arrays.items():
        feed["in_" + name] = a = np.ascontiguousarray(a)
        d[name] = nc.dram_tensor("in_" + name, a.shape, mybir.dt.from_np(a.dtype), kind="ExternalInput").ap()
    d["out"] = nc.dram_tensor("out_h", (NB, SEQ, DM), F32, kind="ExternalOutput").ap()
    build(nc, d)
    return run_bass_kernel_spmd(nc, [feed], core_ids=[0]).results[0]["out_h"]
```
